# Optimizing a Trainium2 kernel written in Bass

```python
import numpy as np
import jax
import jax.numpy as jnp

def _softmax(x, axis=-1):
    return jax.nn.softmax(x, axis=axis)

def _gelu(x):
    return jax.nn.gelu(x, approximate=True)

def _silu(x):
    return jax.nn.silu(x)

def _sigmoid(x):
    return jax.nn.sigmoid(x)

def _layernorm(x, axis=-1, eps=1e-05):
    m = jnp.mean(x, axis=axis, keepdims=True)
    v = jnp.var(x, axis=axis, keepdims=True)
    return (x - m) / jnp.sqrt(v + eps)

def _scatter_add(tgt, idx, src, axis=0):
    return tgt.at[idx].add(src)

def _segment_sum(src, seg, n):
    return jax.ops.segment_sum(src, seg, n)
kernel_name = 'mk_perceiver_d1_seqx_r4_036f2e'

def setup_inputs(seed: int=0):
    np.random.seed(seed)
    _w = jnp.asarray

    def _rec_inputs():
        import jax
        import jax.numpy as jnp
        _rk = jax.random.key(seed)
        x = -0.0003929 + 0.9999 * jax.random.normal(jax.random.fold_in(_rk, 1), (1, 128, 512), jnp.float32)
        _lenS = 128 - jax.random.randint(jax.random.fold_in(_rk, 7), (1,), 0, max(1, 128 // 4) + 1, jnp.int32)
        _lenS2 = 12544 - jax.random.randint(jax.random.fold_in(_rk, 8), (1,), 0, max(1, 12544 // 4) + 1, jnp.int32)
        _ctx_2048P = jax.random.normal(jax.random.fold_in(_rk, 11), (1, 16, 512), jnp.float32)
        _ctx_2048c = jax.random.dirichlet(jax.random.fold_in(_rk, 511), 0.3 * jnp.ones((16,), jnp.float32), (1, 12544))
        _ctx_2048t = jnp.einsum('bsk,bkd->bsd', _ctx_2048c, _ctx_2048P)
        _ctx_2048t = _ctx_2048t * jax.lax.rsqrt(jnp.mean(jnp.square(_ctx_2048t)) + 1e-12) * 0.953939
        ctx_2048 = -0.000514642 + 1.00011 * (_ctx_2048t + 0.3 * jax.random.normal(jax.random.fold_in(_rk, 611), (1, 12544, 512), jnp.float32))
        _validS = jnp.arange(128)[None, :] < _lenS[:, None]
        _validS2 = jnp.arange(12544)[None, :] < _lenS2[:, None]
        _causal = jnp.tril(jnp.ones((128, 128), dtype=bool))
        mask_BxSxS2_ff0 = jnp.where(jnp.ones((1, 128, 12544), dtype=bool), 0.0, -1000000000.0).astype(jnp.float32)
        return (x, ctx_2048, mask_BxSxS2_ff0)
    x, ctx_2048, mask_BxSxS2_ff0 = _rec_inputs()

    def _L0_xattn_setup():
        import jax, jax.numpy as jnp
        import numpy as np
        NUM_HEADS = 16
        EPS = 1e-08

        def _dyn_quant(x):
            s = jnp.maximum(jnp.max(jnp.abs(x), axis=-1, keepdims=True) / 127.0, EPS)
            q = jnp.clip(jnp.round(x / s), -127.0, 127.0)
            return (q, s)

        def _quant_weight(w):
            s = jnp.maximum(jnp.max(jnp.abs(w), axis=1, keepdims=True) / 127.0, EPS)
            q = jnp.clip(jnp.round(w / s), -127.0, 127.0)
            return (q, s)

        def _w8a8_linear(x, w, b):
            qx, sx = _dyn_quant(x)
            qw, sw = _quant_weight(w)
            y = jnp.einsum('bnc,oc->bno', qx, qw) * (sx * sw[:, 0])
            return y + b
        key = jax.random.key(seed)
        ks = jax.random.split(key, 9)
        B, N, L, C = (2, 1024, 128, 512)
        sc = 0.02
        return {'x': jax.random.normal(ks[0], (B, N, C), jnp.float32), 'cond': jax.random.normal(ks[1], (B, L, C), jnp.float32), 'mask': jnp.zeros((B, N, L), jnp.float32), 'wq': jax.random.normal(ks[2], (C, C), jnp.float32) * sc, 'bq': jnp.zeros((C,), jnp.float32), 'wk': jax.random.normal(ks[3], (C, C), jnp.float32) * sc, 'bk': jnp.zeros((C,), jnp.float32), 'wv': jax.random.normal(ks[4], (C, C), jnp.float32) * sc, 'bv': jnp.zeros((C,), jnp.float32), 'wo': jax.random.normal(ks[5], (C, C), jnp.float32) * sc, 'bo': jnp.zeros((C,), jnp.float32)}
    _L0_xattn_all = _L0_xattn_setup()
    _L0_xattn_in = {k: v for k, v in _L0_xattn_all.items() if k in ('wq', 'bq', 'wk', 'bk', 'wv', 'bv', 'wo', 'bo')}
    del _L0_xattn_all

    def _L0_attn_setup():
        import jax, jax.numpy as jnp
        import numpy as np
        D = 512
        H = 8
        CHUNK = 128
        NORM_GK = 16.0
        EPS = 1e-05

        def _chunked_gla(q, k, v, gk):
            gkc = jnp.cumsum(gk, axis=-2)
            qd = q * jnp.exp(gkc)
            kd = k * jnp.exp(gkc[..., -1:, :] - gkc)
            A = jnp.einsum('bhnid,bhnjd->bhnij', qd, k * jnp.exp(-gkc))
            c = q.shape[-2]
            mask = jnp.tril(jnp.ones((c, c), dtype=bool))
            o_intra = jnp.einsum('bhnij,bhnjv->bhniv', jnp.where(mask, A, 0.0), v)
            decay_last = jnp.exp(gkc[..., -1, :])

            def step(S, inp):
                qd_c, kd_c, v_c, dl = inp
                o1 = jnp.einsum('bhcd,bhdv->bhcv', qd_c, S)
                S = dl[..., :, None] * S + jnp.einsum('bhcd,bhcv->bhdv', kd_c, v_c)
                return (S, o1)
            b, h, n, _, dk = q.shape
            dv = v.shape[-1]
            S0 = jnp.zeros((b, h, dk, dv), q.dtype)
            xs = (jnp.moveaxis(qd, 2, 0), jnp.moveaxis(kd, 2, 0), jnp.moveaxis(v, 2, 0), jnp.moveaxis(decay_last, 2, 0))
            _, o_inter = jax.lax.scan(step, S0, xs)
            o_inter = jnp.moveaxis(o_inter, 0, 2)
            return o_inter + o_intra
        key = jax.random.key(seed)
        ks = jax.random.split(key, 10)
        s = 0.02
        return {'x': jax.random.normal(ks[0], (4, 512, D), jnp.float32), 'Wq': jax.random.normal(ks[1], (D, D // 2), jnp.float32) * s, 'Wk': jax.random.normal(ks[2], (D, D // 2), jnp.float32) * s, 'Wkg1': jax.random.normal(ks[3], (D, 16), jnp.float32) * s, 'Wkg2': jax.random.normal(ks[4], (16, D // 2), jnp.float32) * s, 'bkg2': jnp.zeros((D // 2,), jnp.float32), 'Wv': jax.random.normal(ks[5], (D, D), jnp.float32) * s, 'Wg': jax.random.normal(ks[6], (D, D), jnp.float32) * s, 'bg': jnp.zeros((D,), jnp.float32), 'Wo': jax.random.normal(ks[7], (D, D), jnp.float32) * s}
    _L0_attn_all = _L0_attn_setup()
    _L0_attn_in = {k: v for k, v in _L0_attn_all.items() if k in ('Wq', 'Wk', 'Wkg1', 'Wkg2', 'bkg2', 'Wv', 'Wg', 'bg', 'Wo')}
    del _L0_attn_all

    def _L0_ffn_setup():
        import jax, jax.numpy as jnp
        import numpy as np
        H = 512
        I = 256
        E = 16
        K = 2
        B, S = (4, 256)
        key = jax.random.key(seed)
        ks = jax.random.split(key, 5)
        scale = 0.02
        x = jax.random.normal(ks[0], (B, S, H), dtype=jnp.float32)
        gate_w = jax.random.normal(ks[1], (E, H), dtype=jnp.float32) * scale
        wg = jax.random.normal(ks[2], (E, H, I), dtype=jnp.float32) * scale
        wu = jax.random.normal(ks[3], (E, H, I), dtype=jnp.float32) * scale
        wd = jax.random.normal(ks[4], (E, I, H), dtype=jnp.float32) * scale
        return {'x': x, 'gate_w': gate_w, 'wg': wg, 'wu': wu, 'wd': wd}
    _L0_ffn_all = _L0_ffn_setup()
    _L0_ffn_in = {k: v for k, v in _L0_ffn_all.items() if k in ('gate_w', 'wg', 'wu', 'wd')}
    del _L0_ffn_all
    return {'x': x, 'ctx_2048': ctx_2048, 'mask_BxSxS2_ff0': mask_BxSxS2_ff0, 'L0_xattn_wq': _L0_xattn_in['wq'], 'L0_xattn_bq': _L0_xattn_in['bq'], 'L0_xattn_wk': _L0_xattn_in['wk'], 'L0_xattn_bk': _L0_xattn_in['bk'], 'L0_xattn_wv': _L0_xattn_in['wv'], 'L0_xattn_bv': _L0_xattn_in['bv'], 'L0_xattn_wo': _L0_xattn_in['wo'], 'L0_xattn_bo': _L0_xattn_in['bo'], 'L0_attn_Wq': _L0_attn_in['Wq'], 'L0_attn_Wk': _L0_attn_in['Wk'], 'L0_attn_Wkg1': _L0_attn_in['Wkg1'], 'L0_attn_Wkg2': _L0_attn_in['Wkg2'], 'L0_attn_bkg2': _L0_attn_in['bkg2'], 'L0_attn_Wv': _L0_attn_in['Wv'], 'L0_attn_Wg': _L0_attn_in['Wg'], 'L0_attn_bg': _L0_attn_in['bg'], 'L0_attn_Wo': _L0_attn_in['Wo'], 'L0_ffn_gate_w': _L0_ffn_in['gate_w'], 'L0_ffn_wg': _L0_ffn_in['wg'], 'L0_ffn_wu': _L0_ffn_in['wu'], 'L0_ffn_wd': _L0_ffn_in['wd']}

def reference(x, ctx_2048, mask_BxSxS2_ff0, L0_xattn_wq, L0_xattn_bq, L0_xattn_wk, L0_xattn_bk, L0_xattn_wv, L0_xattn_bv, L0_xattn_wo, L0_xattn_bo, L0_attn_Wq, L0_attn_Wk, L0_attn_Wkg1, L0_attn_Wkg2, L0_attn_bkg2, L0_attn_Wv, L0_attn_Wg, L0_attn_bg, L0_attn_Wo, L0_ffn_gate_w, L0_ffn_wg, L0_ffn_wu, L0_ffn_wd):
    import jax
    import jax.numpy as jnp

    def _L0_xattn_ref(x, cond, mask, wq, bq, wk, bk, wv, bv, wo, bo):
        import jax, jax.numpy as jnp
        import numpy as np
        NUM_HEADS = 16
        EPS = 1e-08

        def _dyn_quant(x):
            s = jnp.maximum(jnp.max(jnp.abs(x), axis=-1, keepdims=True) / 127.0, EPS)
            q = jnp.clip(jnp.round(x / s), -127.0, 127.0)
            return (q, s)

        def _quant_weight(w):
            s = jnp.maximum(jnp.max(jnp.abs(w), axis=1, keepdims=True) / 127.0, EPS)
            q = jnp.clip(jnp.round(w / s), -127.0, 127.0)
            return (q, s)

        def _w8a8_linear(x, w, b):
            qx, sx = _dyn_quant(x)
            qw, sw = _quant_weight(w)
            y = jnp.einsum('bnc,oc->bno', qx, qw) * (sx * sw[:, 0])
            return y + b
        B, N, C = x.shape
        L = cond.shape[1]
        H = NUM_HEADS
        D = C // H
        inv_sqrt_d = np.float32(1.0 / np.sqrt(D))
        q = _w8a8_linear(x, wq, bq).reshape(B, N, H, D).transpose(0, 2, 1, 3)
        k = (cond @ wk.T + bk).reshape(B, L, H, D).transpose(0, 2, 1, 3)
        v = (cond @ wv.T + bv).reshape(B, L, H, D).transpose(0, 2, 1, 3)
        scores = jnp.einsum('bhnd,bhld->bhnl', q, k) * inv_sqrt_d + mask[:, None]
        attn = jax.nn.softmax(scores, axis=-1)
        o = jnp.einsum('bhnl,bhld->bhnd', attn, v)
        o = o.transpose(0, 2, 1, 3).reshape(B, N, C)
        return _w8a8_linear(o, wo, bo)

    def _L0_attn_ref(x, Wq, Wk, Wkg1, Wkg2, bkg2, Wv, Wg, bg, Wo):
        import jax, jax.numpy as jnp
        import numpy as np
        D = 512
        H = 8
        CHUNK = 128
        NORM_GK = 16.0
        EPS = 1e-05

        def _chunked_gla(q, k, v, gk):
            gkc = jnp.cumsum(gk, axis=-2)
            qd = q * jnp.exp(gkc)
            kd = k * jnp.exp(gkc[..., -1:, :] - gkc)
            A = jnp.einsum('bhnid,bhnjd->bhnij', qd, k * jnp.exp(-gkc))
            c = q.shape[-2]
            mask = jnp.tril(jnp.ones((c, c), dtype=bool))
            o_intra = jnp.einsum('bhnij,bhnjv->bhniv', jnp.where(mask, A, 0.0), v)
            decay_last = jnp.exp(gkc[..., -1, :])

            def step(S, inp):
                qd_c, kd_c, v_c, dl = inp
                o1 = jnp.einsum('bhcd,bhdv->bhcv', qd_c, S)
                S = dl[..., :, None] * S + jnp.einsum('bhcd,bhcv->bhdv', kd_c, v_c)
                return (S, o1)
            b, h, n, _, dk = q.shape
            dv = v.shape[-1]
            S0 = jnp.zeros((b, h, dk, dv), q.dtype)
            xs = (jnp.moveaxis(qd, 2, 0), jnp.moveaxis(kd, 2, 0), jnp.moveaxis(v, 2, 0), jnp.moveaxis(decay_last, 2, 0))
            _, o_inter = jax.lax.scan(step, S0, xs)
            o_inter = jnp.moveaxis(o_inter, 0, 2)
            return o_inter + o_intra
        b, T, _ = x.shape
        n = T // CHUNK
        dk = D // 2 // H
        dv = D // H
        scaling = (D // H) ** (-0.5)
        q = x @ Wq
        k = x @ Wk * scaling
        gk = jax.nn.log_sigmoid(x @ Wkg1 @ Wkg2 + bkg2) / NORM_GK
        v = x @ Wv
        g = x @ Wg + bg

        def split(t, hd):
            return t.reshape(b, n, CHUNK, H, hd).transpose(0, 3, 1, 2, 4)
        o = _chunked_gla(split(q, dk), split(k, dk), split(v, dv), split(gk, dk))
        mu = o.mean(-1, keepdims=True)
        var = o.var(-1, keepdims=True)
        o = (o - mu) / jnp.sqrt(var + EPS)
        o = o.transpose(0, 2, 3, 1, 4).reshape(b, T, D)
        o = jax.nn.silu(g) * o
        return o @ Wo

    def _L0_ffn_ref(x, gate_w, wg, wu, wd):
        import jax, jax.numpy as jnp
        import numpy as np
        H = 512
        I = 256
        E = 16
        K = 2
        B, S = (4, 256)
        b, s, h = x.shape
        xf = x.reshape(-1, h)
        T = xf.shape[0]
        scores = jax.nn.softmax(xf @ gate_w.T, axis=-1)
        topk_w, topk_idx = jax.lax.top_k(scores, K)
        topk_w = topk_w / (jnp.sum(topk_w, axis=-1, keepdims=True) + 1e-20)
        combine = jnp.zeros((T, E), dtype=xf.dtype).at[jnp.arange(T)[:, None], topk_idx].add(topk_w)
        g = jnp.einsum('th,ehi->tei', xf, wg)
        u = jnp.einsum('th,ehi->tei', xf, wu)
        a = jax.nn.silu(g) * u * combine[:, :, None]
        y = jnp.einsum('tei,eih->th', a, wd)
        return y.reshape(b, s, h)
    x = x + _L0_xattn_ref(_layernorm(x, axis=-1), ctx_2048, mask_BxSxS2_ff0, L0_xattn_wq, L0_xattn_bq, L0_xattn_wk, L0_xattn_bk, L0_xattn_wv, L0_xattn_bv, L0_xattn_wo, L0_xattn_bo)
    x = x + _L0_attn_ref(_layernorm(x, axis=-1), L0_attn_Wq, L0_attn_Wk, L0_attn_Wkg1, L0_attn_Wkg2, L0_attn_bkg2, L0_attn_Wv, L0_attn_Wg, L0_attn_bg, L0_attn_Wo)
    x = x + _L0_ffn_ref(_layernorm(x, axis=-1), L0_ffn_gate_w, L0_ffn_wg, L0_ffn_wu, L0_ffn_wd)
    return x

_drawn_inputs = setup_inputs


def setup_inputs(seed=0):
    import zlib

    import numpy as np

    out = dict(_drawn_inputs(seed))
    spreads = {'L0_xattn_bq': (0.0, 0.8),
     'L0_xattn_bk': (0.0, 0.8),
     'L0_xattn_bv': (0.0, 0.1),
     'L0_xattn_bo': (0.0, 0.1),
     'L0_attn_bkg2': (0.0, 0.8),
     'L0_attn_bg': (0.0, 0.333)}
    factors = {'L0_xattn_wq': 7.89, 'L0_xattn_wk': 7.685, 'L0_attn_Wkg1': 8.0, 'L0_attn_Wkg2': 8.0}
    for name, (base, spread) in spreads.items():
        noise = np.random.default_rng([zlib.crc32(name.encode()), seed]).standard_normal(out[name].shape)
        drawn = base * np.exp(spread * noise) if base else spread * noise
        out[name] = jnp.asarray(drawn.astype(out[name].dtype))
    for name, factor in factors.items():
        out[name] = (out[name] * factor).astype(out[name].dtype)
    return out
```

```python
from contextlib import ExitStack

import concourse.bass as bass
from concourse import mybir

ALU = mybir.AluOpType
ACT = mybir.ActivationFunctionType
AX = mybir.AxisListType
F32 = mybir.dt.float32
F32R = mybir.dt.float32r
BF16 = mybir.dt.bfloat16
U32 = mybir.dt.uint32

P = 128
T = 128
C = 512
CC = C // P
L = 12544
H = 16
D = C // H
G = 4
HG = H // G
KB = 512
KB0 = 256
NB = (L - KB0) // KB + 1
NT = KB // P
LOOP_PERIODS = (NB - 3) // 2
SLOTS = 8

GH = 8
GK = C // 2 // GH
GV = C // GH
GKT = C // 2 // P
E = 16
I = 256
EPS_LN = 1e-5
EPS_Q = 1e-8
QMAX = 127.0
ROUND = 12582912.0
BIG = 3.0e38
EXPERT_SLOTS = 11
CHUNKS_IN = ((), (0, 1), (2,), (3,))


def block_tiles(s):
    return KB0 // P if isinstance(s, int) and s == 0 else NT


def tiles_before(s):
    return 0 if isinstance(s, int) and s == 0 else NT * s - (NT - KB0 // P)


def perceiver_kernel(nc, x, ctx_first, ctx_rest, mask, wq, bq, wkT, bk, wvT, bv, wo, bo,
                     g_wq, g_wk, g_wkg1, g_wkg2, g_bkg2, g_wv, g_wg, g_bg, g_wo,
                     gateT, wg, wu, wd, eye, upper, expert_ids, out):
    ctx = ExitStack()
    with ctx:
        def sb(name, shape, dt=F32, where=ctx):
            return where.enter_context(nc.sbuf_tensor(name, shape, dt))

        def sem(name):
            return ctx.enter_context(nc.semaphore(name))

        x_sb = sb("x_sb", [P, C])
        ident = sb("ident", [P, P])
        ident_bf = sb("ident_bf", [P, P], BF16)
        woT = sb("woT", [P, CC, C], BF16)
        wo_scale_b = sb("wo_scale_b", [P, C])
        bo_b = sb("bo_b", [P, C])
        acc = sb("acc", [P, G, T])
        l_sum = sb("l_sum", [P, H])
        col = sb("col", [P, 64])
        stats = sb("stats", [P, 6])

        att = ExitStack()
        wk_hi = sb("wk_hi", [P, CC, C], F32R, att)
        wk_lo = sb("wk_lo", [P, CC, C], F32R, att)
        wv_hi = sb("wv_hi", [P, CC, C], F32R, att)
        wv_lo = sb("wv_lo", [P, CC, C], F32R, att)
        c_hi = [sb(f"c_hi{i}", [P, CC, KB], F32R, att) for i in range(2)]
        c_lo = [sb(f"c_lo{i}", [P, CC, KB], F32R, att) for i in range(2)]
        raw = [sb(f"raw{i}", [P, CC, KB], F32, att) for i in range(2)]
        v_sb = [sb(f"v_sb{i}", [P, NT, C], F32, att) for i in range(2)]
        k_stack = sb("k_stack", [96, H, KB], F32R, att)
        q_stack = sb("q_stack", [96, H, T], F32R, att)
        k_hi = [sb(f"k_hi{i}", [P, KB], F32R, att) for i in range(2)]
        k_lo = [sb(f"k_lo{i}", [P, KB], F32R, att) for i in range(2)]
        mask_sb = [sb(f"mask_sb{i}", [P, KB], F32, att) for i in range(2)]
        neg_max = [sb(f"neg_max{i}", [P, H], F32, att) for i in range(2)]
        row_sum = [sb(f"row_sum{i}", [P, H], F32, att) for i in range(2)]
        drop = sb("drop", [P, H], F32, att)
        rescale_w = sb("rescale_w", [P, H, D], F32, att)
        bv_b = sb("bv_b", [P, C], F32, att)
        bq_c = sb("bq_c", [P, G], F32, att)
        bk_c = sb("bk_c", [P, G], F32, att)

        wq_nat = raw[1]
        wq_rnd = v_sb[1]
        wk_nat = v_sb[0]
        att_end = ExitStack()
        wv_nat = sb("wv_nat", [P, CC, C], F32, att_end)
        wqT = sb("wqT", [P, CC, C], BF16, att_end)
        wq_q = sb("wq_q", [P, CC, C], BF16, att_end)
        xq = sb("xq", [P, C], BF16, att_end)
        xqT = sb("xqT", [P, CC, T], BF16, att_end)
        x_norm = sb("x_norm", [P, C], F32, att_end)
        x_scale_w = sb("x_scale_w", [P, P], F32, att_end)
        q_sb = sb("q_sb", [P, G, T], F32, att_end)
        x_scale_b = x_norm[:, 0:T]
        q_hi = sb("q_hi", [P, G, T], F32R, att_end)
        q_lo = sb("q_lo", [P, G, T], F32R, att_end)
        att_end.close()
        wo_nat = raw[0]
        wo_rnd = raw[1]
        wo_q = raw[0][:, 0:2, :].bitcast(BF16).rearrange("p a b -> p (a b)").rearrange("p (c i) -> p c i", c=CC)
        wo_scale_w = raw[0][:, 2, :].rearrange("p (c t) -> p c t", c=CC)
        prob = sb("prob", [P, SLOTS, KB], F32, att)
        probT = sb("probT", [P, NT, HG * T], F32, att)
        att.close()

        w_gq = sb("w_gq", [P, CC, C // 2])
        w_gk = sb("w_gk", [P, CC, C // 2])
        w_gv = sb("w_gv", [P, CC, C])
        w_gg = sb("w_gg", [P, CC, C])
        w_go = sb("w_go", [P, CC, C])
        experts_at = [sb(f"expert{i}", [P, 3, 1024]) for i in range(EXPERT_SLOTS)]
        w_kg1 = sb("w_kg1", [P, CC, 16])
        w_kg2 = sb("w_kg2", [16, C // 2])
        bkg2_b = sb("bkg2_b", [P, C // 2])
        bg_b = sb("bg_b", [P, C])
        upper_sb = sb("upper_sb", [P, P])
        gate_sb = sb("gate_sb", [P, CC, E])
        ids_sb = sb("ids_sb", [P, E])
        t0 = sb("t0", [P, C])
        t1 = sb("t1", [P, C])
        t2 = sb("t2", [P, C])
        t3 = sb("t3", [P, C])
        v_gla = sb("v_gla", [P, C])
        xT = sb("xT", [P, CC, T])
        o_q = sb("o_q", [P, C], BF16)
        o_qT = sb("o_qT", [P, CC, T], BF16)
        small = sb("small", [P, 8, E])
        top_ids = sb("top_ids", [P, 8], U32)
        at_sb = sb("at_sb", [P, GH, T])
        act_e = [sb(f"act_e{i}", [P, I]) for i in range(2)]
        silu_e = [sb(f"silu_e{i}", [P, I]) for i in range(2)]
        act_eT = [sb(f"act_eT{i}", [P, I // P, T]) for i in range(2)]

        names = ["s0", "s1", "t0", "t1", "k", "v", "o", "a"]
        bank = {n: ctx.enter_context(nc.psum_tensor(f"bank_{n}", [P, 512], F32)) for n in names}
        ps_s = [bank["s0"], bank["s1"]]
        ps_t = [bank["t0"], bank["t1"]]

        x_landed = sem("x_landed")
        wq_landed = sem("wq_landed")
        wo_landed = sem("wo_landed")
        const_landed = sem("const_landed")
        bias_landed = sem("bias_landed")
        wk_landed = sem("wk_landed")
        wv_landed = sem("wv_landed")
        w_hi_ready = sem("w_hi_ready")
        w_lo_ready = sem("w_lo_ready")
        ctx_landed = [sem(f"ctx_landed{i}") for i in range(2)]
        mask_landed = [sem(f"mask_landed{i}") for i in range(2)]
        ctx_hi_ready = sem("ctx_hi_ready")
        ctx_lo_ready = sem("ctx_lo_ready")
        ident_ready = sem("ident_ready")
        quant_ready = sem("quant_ready")
        quant_turned = sem("quant_turned")
        turned_kept = sem("turned_kept")
        wo_ready = sem("wo_ready")
        wq_free = sem("wq_free")
        q_made = sem("q_made")
        q_ready = sem("q_ready")
        q_hi_ready = sem("q_hi_ready")
        q_lo_ready = sem("q_lo_ready")
        q_landed = sem("q_landed")
        init_ready = sem("init_ready")

        k_projected = sem("k_projected")
        v_projected = sem("v_projected")
        k_hi_ready = sem("k_hi_ready")
        k_lo_ready = sem("k_lo_ready")
        k_landed = [sem(f"k_landed{g}") for g in range(G)]
        v_ready = sem("v_ready")
        scored = sem("scored")
        masked = sem("masked")
        drop_ready = sem("drop_ready")
        prob_ready = sem("prob_ready")
        turned = sem("turned")
        kept_even = sem("kept_even")
        kept_odd = sem("kept_odd")
        group_applied = sem("group_applied")
        rescale_ready = sem("rescale_ready")
        rescale_turned = sem("rescale_turned")
        scaled = sem("scaled")
        folded = sem("folded")
        sums_scaled = sem("sums_scaled")

        dve_chain = sem("dve_chain")
        pe_done = sem("pe_done")
        act_done = sem("act_done")
        pool_done = sem("pool_done")
        dve_done = sem("dve_done")
        gla_landed = sem("gla_landed")
        tail_landed = sem("tail_landed")
        expert_landed = [sem(f"expert_landed{i}") for i in range(EXPERT_SLOTS)]
        up_done = sem("up_done")
        silu_done = sem("silu_done")
        act_ready = sem("act_ready")
        act_turned = sem("act_turned")
        act_kept = sem("act_kept")
        down_done = sem("down_done")
        out_ready = sem("out_ready")
        var_ready = sem("var_ready")
        std_ready = sem("std_ready")
        abs_ready = sem("abs_ready")
        exp_neg = sem("exp_neg")
        ln_ready = sem("ln_ready")
        decay_ready = sem("decay_ready")
        gate_ready = sem("gate_ready")
        silu_ready = sem("silu_ready")
        scores_kept = sem("scores_kept")
        logit_ready = sem("logit_ready")
        route_ready = sem("route_ready")
        one_c = col[:, 50:51]
        out_landed = sem("out_landed")

        STACKED = 12 * 16

        def par(p, ph):
            return p, ph

        def keys_bank(s, g):
            if isinstance(s, int) and s == 0:
                return bank[("k", "v", "o", "a")[g]][:, 0:KB0]
            return bank["k"][:, :]

        def values_bank(s, t):
            if isinstance(s, int) and s == 0:
                return bank[("v", "t1")[t]][:, :]
            return bank["v"][:, :]

        def heads_of_row(r, j):
            return q_stack[r * D:(r + 1) * D, :, :].rearrange("d (g j) t -> d g j t", j=HG)[:, :, j, :]

        block = ctx.enter_context(nc.Block())

        @block.sync
        def _(sp):
            def load_ctx(at, parity):
                if at is None:
                    sp.dma_start(raw[0][:, :, 0:KB0], ctx_first).then_inc(ctx_landed[0], 16)
                else:
                    sp.dma_start(raw[parity][:, :, :], ctx_rest[at]).then_inc(ctx_landed[parity], 16)

            def load_mask(at, parity):
                if isinstance(at, int) and at == 0:
                    sp.dma_start(mask_sb[0][:, 0:KB0], mask[:, 0:KB0]).then_inc(mask_landed[0], 16)
                else:
                    sp.dma_start(mask_sb[parity][:, :], mask[:, bass.ds(at, KB)])\
                      .then_inc(mask_landed[parity], 16)

            def stack_keys(g, width, made):
                sp.wait_ge(k_hi_ready, made)
                sp.wait_ge(k_lo_ready, made)
                for j in range(HG):
                    for r, part in enumerate((k_hi, k_lo, k_hi)):
                        sp.dma_start(k_stack[r * D:(r + 1) * D, HG * g + j, 0:width].bitcast(F32),
                                     part[g % 2][j * D:(j + 1) * D, 0:width].bitcast(F32))\
                          .then_inc(k_landed[g], 16)

            def period(p, half, parity, load=True, project=True):
                value = sp.snap if not isinstance(p, int) else int
                split_before = value(CC * (p + 2))
                block_at = value(p + 2)
                mask_at = value(KB * (p + 1) + KB0)
                masks_before = value(H * (p + 1))
                keys_made = [value(G * (p + 1) + q + 1) for q in range(G)]
                for q in range(G):
                    if q == 3 and load:
                        sp.wait_ge(ctx_lo_ready, split_before)
                        sp.wait_ge(ctx_hi_ready, split_before)
                        load_ctx(block_at, 1 - parity)
                    if project:
                        stack_keys(q, KB, keys_made[q])
                    if q == 3 and project and not (isinstance(p, int) and p + 2 >= NB):
                        sp.wait_ge(masked, masks_before)
                        load_mask(mask_at, parity)

            sp.dma_start(x_sb[:, :], x).then_inc(x_landed, 16)
            load_ctx(None, 0)
            sp.dma_start(wk_nat[:, :, :], wkT).then_inc(wk_landed, 16)
            sp.dma_start(raw[1][:, :, :], wq).then_inc(wq_landed, 16)
            sp.dma_start(ident[:, :], eye).then_inc(const_landed, 16)
            sp.dma_start(wv_nat[:, :, :], wvT).then_inc(wv_landed, 16)
            for where, what in ((bq_c[:, :], bq), (bk_c[:, :], bk), (bv_b[:, :], bv.partition_broadcast(P)),
                                (bo_b[:, :], bo.partition_broadcast(P))):
                sp.dma_start(where, what).then_inc(bias_landed, 16)
            load_mask(0, 0)
            load_mask(KB0, 1)
            sp.wait_ge(wq_free, 1)
            load_ctx(0, 1)
            sp.wait_ge(ctx_lo_ready, CC)
            sp.wait_ge(ctx_hi_ready, CC)
            load_ctx(1, 0)

            period(0, 0, 0)
            with sp.Fori(0, LOOP_PERIODS - 1) as i:
                period(2 * i + 1, i, 1)
                period(2 * i + 2, i + 1, 0)
            period(NB - 4, (NB - 4) // 2, (NB - 4) % 2)
            period(NB - 3, (NB - 3) // 2, (NB - 3) % 2, load=False)
            sp.wait_ge(ctx_hi_ready, CC * NB)
            sp.wait_ge(ctx_lo_ready, CC * NB)
            sp.dma_start(wo_nat[:, :, :], wo).then_inc(wo_landed, 16)
            period(NB - 2, (NB - 2) // 2, (NB - 2) % 2, load=False)

            sp.wait_ge(k_projected, G * NB)
            sp.wait_ge(v_projected, tiles_before(NB))
            for where, what in ((w_gv, g_wv), (w_gg, g_wg), (w_go, g_wo), (w_gq, g_wq), (w_gk, g_wk)):
                sp.dma_start(where[:, :, :], what.rearrange("(c p) n -> p c n", p=P)).then_inc(gla_landed, 16)

            def load_expert(e):
                at = experts_at[e % EXPERT_SLOTS]
                for n, w in enumerate((wg, wu, wd)):
                    sp.dma_start(at[:, n, :].rearrange("p (c i) -> p c i", c=4 if n < 2 else 2),
                                 w[e].rearrange("(c p) i -> p c i", p=P))\
                      .then_inc(expert_landed[e % EXPERT_SLOTS], 16)

            for e in range(2):
                load_expert(e)
            sp.wait_ge(quant_turned, 4)
            for e in range(2, 4):
                load_expert(e)
            sp.wait_ge(folded, NB)
            sp.wait_ge(kept_even, tiles_before(NB) * G // 2)
            for where, what in ((w_kg1[:, :, :], g_wkg1), (w_kg2[:, :], g_wkg2),
                                (bkg2_b[:, :], g_bkg2.partition_broadcast(P)),
                                (bg_b[:, :], g_bg.partition_broadcast(P)), (upper_sb[:, :], upper),
                                (gate_sb[:, :, :], gateT), (ids_sb[:, :], expert_ids.partition_broadcast(P))):
                sp.dma_start(where, what).then_inc(tail_landed, 16)
            for e in range(4, EXPERT_SLOTS):
                load_expert(e)
            for e in range(EXPERT_SLOTS, E):
                sp.wait_ge(down_done, e - EXPERT_SLOTS + 1)
                load_expert(e)
            sp.wait_ge(out_ready, 1)
            sp.dma_start(out, t0[:, :]).then_inc(out_landed, 16)
            sp.wait_ge(out_landed, 16)

        @block.tensor
        def _(pe):
            def project_keys(s, g, part):
                width = KB0 if isinstance(s, int) and s == 0 else KB
                slot = project_slot[0]
                if part == 0:
                    if g == 0:
                        pe.wait_ge(ctx_hi_ready, CC * (s + 1))
                        pe.wait_ge(ctx_lo_ready, CC * (s + 1))
                    if isinstance(s, int) and s == 1 and g == 0:
                        pe.wait_ge(k_lo_ready, 1)
                    elif not (isinstance(s, int) and s == 0):
                        pe.wait_ge(k_lo_ready, G * s + g)
                steps = [(c, a, b) for c in range(CC)
                         for a, b in ((wk_hi, c_hi[slot]), (wk_hi, c_lo[slot]), (wk_lo, c_hi[slot]))]
                for n in range(part * 6, part * 6 + 6):
                    c, a, b = steps[n]
                    mm = nc.tensor.matmul(keys_bank(s, g), a[:, c, g * P:(g + 1) * P],
                                          b[:, c, 0:width], start=(n == 0), stop=(n == 11))
                if part == 1:
                    mm.then_inc(k_projected, 1)

            def project_values(s, t, part):
                slot = project_slot[0]
                if part == 0 and not (isinstance(s, int) and s == 0):
                    pe.wait_ge(v_ready, tiles_before(s) + t)
                steps = [(c, a, b) for c in range(CC)
                         for a, b in ((c_hi[slot], wv_hi), (c_hi[slot], wv_lo), (c_lo[slot], wv_hi))]
                for n in range(part * 6, part * 6 + 6):
                    c, a, b = steps[n]
                    mm = nc.tensor.matmul(values_bank(s, t), a[:, c, t * P:(t + 1) * P], b[:, c, :],
                                          start=(n == 0), stop=(n == 11))
                if part == 1:
                    mm.then_inc(v_projected, 1)

            def score_pair(s, g, j):
                width = KB0 if isinstance(s, int) and s == 0 else KB
                n = H * s + HG * g + j
                if not (isinstance(n, int) and n == 0):
                    pe.wait_ge(masked, n)
                if j == 0:
                    pe.wait_ge(k_landed[g], STACKED * (s + 1))
                for h in (j, j + 1):
                    nc.tensor.matmul(ps_s[h % 2][:, 0:width], q_stack[:, HG * g + h, :],
                                     k_stack[:, HG * g + h, 0:width], start=True, stop=True).then_inc(scored, 1)

            def turn(s, g, t):
                n = tiles_before(s) * G + g * block_tiles(s) + t
                if t == 0:
                    pe.wait_ge(prob_ready, H * s + HG * (g + 1))
                if not (isinstance(s, int) and s == 0 and g == 0 and t < 2):
                    pe.wait_ge(kept_even if t % 2 == 0 else kept_odd, (n - t % 2) // 2 if isinstance(n, int) else tiles_before(s) * (G // 2) + (g * block_tiles(s) + t - t % 2) // 2)
                if isinstance(s, int) and s == 0 and g == 0 and t == 1:
                    pe.wait_ge(v_ready, KB0 // P)
                for j in range(HG):
                    tr = nc.tensor.transpose(ps_t[t % 2][:, j * T:(j + 1) * T],
                                             prob[:, (HG * g + j) % SLOTS, t * P:(t + 1) * P], ident[:, :])
                tr.then_inc(turned, 1)

            def apply(s, g, t, slot):
                n = tiles_before(s) * (G // 2) + (g * block_tiles(s) + t - t % 2) // 2
                pe.wait_ge(kept_even if t % 2 == 0 else kept_odd, n + 1)
                if t == 0 and g == 0:
                    pe.wait_ge(v_ready, tiles_before(s) + block_tiles(s))
                    if isinstance(s, int) and s == 0:
                        pe.wait_ge(k_lo_ready, G - 1)
                    else:
                        pe.wait_ge(folded, s)
                for j in range(HG):
                    h = HG * g + j
                    mm = nc.tensor.matmul(bank["o"][j * D:(j + 1) * D, g * T:(g + 1) * T],
                                          v_sb[slot][:, t, h * D:(h + 1) * D], probT[:, t, j * T:(j + 1) * T],
                                          start=(t == 0), stop=(t == block_tiles(s) - 1),
                                          tile_position=(0, j * D))
                if t == block_tiles(s) - 1:
                    mm.then_inc(group_applied, 1)

            def period(p, parity, project=True):
                project_slot[0] = (parity + 1) % 2
                nt = block_tiles(p)
                for q in range(G):
                    s, g = (p, q + 1) if q < 3 else (p + 1, 0)
                    if q < 3 or project:
                        score_pair(s, g, 0)
                    if project:
                        project_keys(p + 1, q, 0)
                    turn(p, q, 0)
                    turn(p, q, 1)
                    if project:
                        project_keys(p + 1, q, 1)
                    if q < 3 or project:
                        score_pair(s, g, 2)
                    if q == 0 and not project:
                        pe.wait_ge(turned_kept, 3)
                        for k in range(CC):
                            tr = nc.tensor.transpose(bank["k"][:, k * P:(k + 1) * P], wo_scale_w[:, k, :], ident[:, :])
                        tr.then_inc(quant_turned, 1)
                    apply(p, q, 0, parity)
                    apply(p, q, 1, parity)
                    if project:
                        project_values(p + 1, q, 0)
                    if nt > 2:
                        turn(p, q, 2)
                        turn(p, q, 3)
                    if project:
                        project_values(p + 1, q, 1)
                    if nt > 2:
                        apply(p, q, 2, parity)
                        apply(p, q, 3, parity)
                pe.wait_ge(rescale_ready, p + 1)
                for g in range(G):
                    tr = nc.tensor.transpose(bank["a"][:, g * T:(g + 1) * T],
                                             rescale_w[:, HG * g:HG * (g + 1), :].rearrange("p h d -> p (h d)"),
                                             ident[:, :])
                tr.then_inc(rescale_turned, 1)

            project_slot = [0]

            def turn_weight(w_q, banks):
                for c in range(CC):
                    view = bank[banks[c // 2]][:, :].bitcast(BF16)
                    for k in range(CC):
                        at = (c % 2) * C + k * P
                        tr = nc.tensor.transpose(view[:, at:at + P], w_q[:, k, c * P:(c + 1) * P], ident_bf[:, :])
                return tr

            pe.wait_ge(w_hi_ready, CC)
            pe.wait_ge(w_lo_ready, CC)
            for g in range(2):
                project_keys(0, g, 0)
                project_keys(0, g, 1)
            pe.wait_ge(ident_ready, 1)
            pe.wait_ge(quant_ready, 1)
            xqT_ps = bank["t0"][:, :].bitcast(BF16)
            for c in range(CC):
                nc.tensor.transpose(xqT_ps[:, c * T:(c + 1) * T], xq[:, c * P:(c + 1) * P], ident_bf[:, :])
            nc.tensor.transpose(bank["t1"][:, 0:T], x_scale_w[:, :], ident[:, :]).then_inc(quant_turned, 1)
            pe.wait_ge(quant_ready, 2)
            turn_weight(wq_q, ("s0", "s1")).then_inc(quant_turned, 1)
            project_keys(0, 2, 0)
            project_keys(0, 2, 1)
            pe.wait_ge(turned_kept, 2)
            for g in range(G):
                for c in range(CC):
                    mm = nc.tensor.matmul(bank["t0"][:, g * T:(g + 1) * T], wqT[:, c, g * P:(g + 1) * P],
                                          xqT[:, c, :], start=(c == 0), stop=(c == CC - 1))
            mm.then_inc(q_made, 1)
            project_keys(0, 3, 0)
            project_keys(0, 3, 1)
            pe.wait_ge(w_hi_ready, 2 * CC)
            pe.wait_ge(w_lo_ready, 2 * CC)
            pe.wait_ge(k_lo_ready, 2)
            for t in range(KB0 // P):
                project_values(0, t, 0)
                project_values(0, t, 1)
            pe.wait_ge(q_landed, STACKED)
            score_pair(0, 0, 0)
            score_pair(0, 0, 2)

            period(0, 0)
            with pe.Fori(0, LOOP_PERIODS) as i:
                period(2 * i + 1, 1)
                period(2 * i + 2, 0)
            period(NB - 2, (NB - 2) % 2)
            pe.wait_ge(wo_ready, 1)
            pe.wait_ge(k_lo_ready, G * NB)
            pe.wait_ge(v_ready, tiles_before(NB))
            turn_weight(wo_q, ("k", "v")).then_inc(quant_turned, 1)
            period(NB - 1, (NB - 1) % 2, project=False)

            pe.wait_ge(folded, NB)
            for g in range(G):
                tr = nc.tensor.transpose(bank["t0"][:, g * P:(g + 1) * P], acc[:, g, :], ident[:, :])
            tr.then_inc(pe_done, 1)
            pe.wait_ge(dve_done, 1)
            view = bank["t1"][:, :].bitcast(BF16)
            for c in range(CC):
                tr = nc.tensor.transpose(view[:, c * T:(c + 1) * T], o_q[:, c * P:(c + 1) * P], ident_bf[:, :])
            tr.then_inc(pe_done, 1)
            pe.wait_ge(dve_done, 2)
            for c in range(CC):
                mm = nc.tensor.matmul(bank["s0"][:, :], o_qT[:, c, :], woT[:, c, :], start=(c == 0), stop=(c == CC - 1))
            mm.then_inc(pe_done, 1)

            def turn_x(src, b):
                for c in range(CC):
                    tr = nc.tensor.transpose(bank[b][:, c * T:(c + 1) * T], src[:, c * P:(c + 1) * P], ident[:, :])
                tr.then_inc(pe_done, 1)

            pe.wait_ge(dve_done, 3)
            turn_x(t1, "t0")
            pe.wait_ge(dve_done, 4)
            pe.wait_ge(gla_landed, 16 * 5)
            pe.wait_ge(tail_landed, 16 * 7)
            for c in range(CC):
                mm = nc.tensor.matmul(bank["s0"][0:16, 0:T], w_kg1[:, c, :], xT[:, c, :], start=(c == 0), stop=(c == CC - 1))
            mm.then_inc(pe_done, 1)
            for n, w in enumerate((w_gq, w_gk)):
                for m in range(GKT):
                    for c in range(CC):
                        mm = nc.tensor.matmul(bank["k" if n == 0 else "v"][:, m * T:(m + 1) * T],
                                              w[:, c, m * P:(m + 1) * P], xT[:, c, :], start=(c == 0), stop=(c == CC - 1))
            mm.then_inc(pe_done, 1)
            pe.wait_ge(act_done, 2)
            nc.tensor.matmul(bank["s1"][:, 0:C // 2], t2[0:16, 0:T], w_kg2[:, :], start=True, stop=True)\
              .then_inc(pe_done, 1)
            for c in range(CC):
                mm = nc.tensor.matmul(bank["o"][:, :], xT[:, c, :], w_gv[:, c, :], start=(c == 0), stop=(c == CC - 1))
            mm.then_inc(pe_done, 1)
            for c in range(CC):
                mm = nc.tensor.matmul(bank["a"][:, :], xT[:, c, :], w_gg[:, c, :], start=(c == 0), stop=(c == CC - 1))
            mm.then_inc(pe_done, 1)
            pe.wait_ge(dve_done, 5)
            for m in range(GKT):
                mm = nc.tensor.matmul(bank["t1"][:, m * T:(m + 1) * T], t0[:, m * P:(m + 1) * P], upper_sb[:, :],
                                      start=True, stop=True)
            mm.then_inc(pe_done, 1)
            pe.wait_ge(dve_done, 6)
            for h in range(GH):
                r = (h * GK) % P
                m = h * GK // P
                at = ["s0", "s1", "t0", "t1"][h % 4]
                mm = nc.tensor.matmul(bank[at][:, m * T:(m + 1) * T], t2[r:r + GK, C // 2 + m * T:C // 2 + (m + 1) * T],
                                      t2[r:r + GK, m * T:(m + 1) * T], start=True, stop=True)
            mm.then_inc(pe_done, 1)
            pe.wait_ge(pool_done, 1)
            pe.wait_ge(dve_done, 7)
            for h in range(GH):
                mm = nc.tensor.matmul(bank["k"][:, h * GV:(h + 1) * GV], at_sb[:, h, :], v_gla[:, h * GV:(h + 1) * GV],
                                      start=True, stop=True)
            mm.then_inc(pe_done, 1)
            pe.wait_ge(dve_done, 8)
            turn_x(t0, "v")
            pe.wait_ge(dve_done, 9)
            for c in range(CC):
                mm = nc.tensor.matmul(bank["o"][:, :], xT[:, c, :], w_go[:, c, :], start=(c == 0), stop=(c == CC - 1))
            mm.then_inc(pe_done, 1)

            pe.wait_ge(dve_done, 10)
            turn_x(t1, "t0")
            pe.wait_ge(dve_done, 11)
            for c in range(CC):
                mm = nc.tensor.matmul(bank["t1"][:, 0:E], xT[:, c, :], gate_sb[:, c, :], start=(c == 0), stop=(c == CC - 1))
            mm.then_inc(pe_done, 1)
            nc.tensor.matmul(bank["a"][:, :], ident[:, :], x_sb[:, :], start=True, stop=False)

            def up(e):
                at = experts_at[e % EXPERT_SLOTS]
                pe.wait_ge(expert_landed[e % EXPERT_SLOTS], 48 * (e // EXPERT_SLOTS + 1))
                if e >= 2:
                    pe.wait_ge(act_ready, e - 1)
                b = ps_s[e % 2]
                for n in range(2):
                    w = at[:, n, :].rearrange("p (c i) -> p c i", c=CC)
                    for c in range(CC):
                        mm = nc.tensor.matmul(b[:, n * I:(n + 1) * I], xT[:, c, :], w[:, c, :],
                                              start=(c == 0), stop=(c == CC - 1))
                mm.then_inc(up_done, 1)

            def turn_act(e):
                pe.wait_ge(act_ready, e + 1)
                b = bank["k" if e % 2 == 0 else "v"]
                if e >= 2:
                    pe.wait_ge(act_kept, e - 1)
                for n in range(I // P):
                    tr = nc.tensor.transpose(b[:, n * T:(n + 1) * T], act_e[e % 2][:, n * P:(n + 1) * P], ident[:, :])
                tr.then_inc(act_turned, 1)

            def down(e):
                pe.wait_ge(act_kept, e + 1)
                w = experts_at[e % EXPERT_SLOTS][:, 2, :].rearrange("p (c i) -> p c i", c=I // P)
                for n in range(I // P):
                    mm = nc.tensor.matmul(bank["a"][:, :], act_eT[e % 2][:, n, :], w[:, n, :],
                                          start=False, stop=(e == E - 1 and n == I // P - 1))
                mm.then_inc(down_done, 1)

            for e in range(E + 2):
                if e < E:
                    up(e)
                if e >= 2:
                    down(e - 2)
                if 1 <= e <= E:
                    turn_act(e - 1)

        @block.scalar
        def _(act):
            def split(s, half, slot, c):
                width = KB0 if isinstance(s, int) and s == 0 else KB
                nc.scalar.activation(c_hi[slot][:, c, 0:width], raw[slot][:, c, 0:width], ACT.Copy)\
                  .then_inc(ctx_hi_ready, 1)

            def keys_hi(s, g):
                width = KB0 if isinstance(s, int) and s == 0 else KB
                act.wait_ge(k_projected, G * s + g + 1)
                if g >= 2 or not (isinstance(s, int) and s == 0):
                    act.wait_ge(k_landed[(g - 2) % 4], STACKED * (s + 1) if g >= 2 else STACKED * s)
                nc.scalar.activation(k_hi[g % 2][:, 0:width], keys_bank(s, g), ACT.Identity,
                                     bias=bk_c[:, g:g + 1]).then_inc(k_hi_ready, 1)

            def exponentials(s, g, j, slot):
                width = KB0 if isinstance(s, int) and s == 0 else KB
                h = HG * g + j
                act.wait_ge(masked, H * s + h + 1)
                at = prob[:, h % SLOTS, 0:width]
                nc.scalar.activation(at, at, ACT.Exp, bias=neg_max[slot][:, h:h + 1], scale=-1.0,
                                     accum_out=row_sum[slot][:, h:h + 1]).then_inc(prob_ready, 1)

            def keep(s, g, t):
                n = tiles_before(s) * G + g * block_tiles(s) + t
                act.wait_ge(turned, n + 1)
                nc.scalar.activation(probT[:, t, :], ps_t[0][:, :], ACT.Copy).then_inc(kept_even, 1)

            def period(p, half, parity, project=True, split_next=True):
                nt = block_tiles(p)
                for q in range(G):
                    s, g = (p, q + 1) if q < 3 else (p + 1, 0)
                    slot = parity if q < 3 else (parity + 1) % 2
                    scores = q < 3 or project
                    if split_next:
                        if q == 1:
                            act.wait_ge(k_projected, G * (p + 1))
                            act.wait_ge(v_projected, tiles_before(p) + nt)
                            act.wait_ge(ctx_landed[parity], 16 * (half + 2))
                        for c in CHUNKS_IN[q]:
                            split(p + 2, None, parity, c)
                    if q == 3:
                        if not (isinstance(p, int) and p == 0):
                            act.wait_ge(folded, p)
                        act.wait_ge(drop_ready, (H // 2) * (p + 1))
                        nc.scalar.activation(rescale_w[:, :, :], drop[:, :].unsqueeze(2).to_broadcast([P, H, D]),
                                             ACT.Exp).then_inc(rescale_ready, 1)
                    if scores:
                        exponentials(s, g, 0, slot)
                        exponentials(s, g, 1, slot)
                    keep(p, q, 0)
                    if project:
                        keys_hi(p + 1, q)
                    if scores:
                        exponentials(s, g, 2, slot)
                        exponentials(s, g, 3, slot)
                    if nt > 2:
                        keep(p, q, 2)

            act.wait_ge(dve_chain, 3)
            nc.scalar.activation(col[:, 3:4], col[:, 2:3], ACT.Sqrt).then_inc(act_done, 1)
            act.wait_ge(ctx_landed[0], 16)
            for c in range(CC):
                split(0, 0, 0, c)
            act.wait_ge(wk_landed, 16)
            for c in range(CC):
                nc.scalar.activation(wk_hi[:, c, :], wk_nat[:, c, :], ACT.Copy).then_inc(w_hi_ready, 1)
            act.wait_ge(wv_landed, 16)
            for c in range(CC):
                nc.scalar.activation(wv_hi[:, c, :], wv_nat[:, c, :], ACT.Copy).then_inc(w_hi_ready, 1)
            act.wait_ge(bias_landed, 16 * 4)

            def stack_hi(g, rows):
                act.wait_ge(k_hi_ready, g + 1)
                for j in range(HG):
                    for r in rows:
                        nc.scalar.activation(k_stack[r * D:(r + 1) * D, HG * g + j, 0:KB0],
                                             k_hi[g % 2][j * D:(j + 1) * D, 0:KB0], ACT.Copy)\
                          .then_inc(k_landed[g], 16)

            for g in range(2):
                keys_hi(0, g)
                stack_hi(g, (0, 2))
            act.wait_ge(ctx_landed[1], 16)
            for c in range(CC):
                split(1, 0, 1, c)
            act.wait_ge(q_ready, 1)
            nc.scalar.activation(q_hi[:, :, :], q_sb[:, :, :], ACT.Copy).then_inc(q_hi_ready, 1)
            act.wait_ge(q_hi_ready, 1)
            for j in range(HG):
                nc.scalar.activation(heads_of_row(0, j), q_hi[j * D:(j + 1) * D, :, :], ACT.Copy)\
                  .then_inc(q_landed, 16)
            keys_hi(0, 2)
            for j in range(HG):
                exponentials(0, 0, j, 0)
            stack_hi(2, (0,))
            keys_hi(0, 3)
            stack_hi(3, (0,))

            period(0, 0, 0)
            with act.Fori(0, LOOP_PERIODS) as i:
                period(2 * i + 1, i, 1)
                period(2 * i + 2, i + 1, 0)
            period(NB - 2, (NB - 2) // 2, (NB - 2) % 2, split_next=False)
            period(NB - 1, (NB - 1) // 2, (NB - 1) % 2, project=False, split_next=False)

            def std(n):
                act.wait_ge(dve_done, n)

            act.wait_ge(var_ready, 1)
            nc.scalar.activation(col[:, 3:4], col[:, 2:3], ACT.Sqrt).then_inc(std_ready, 1)
            act.wait_ge(pe_done, 5)
            nc.scalar.activation(t2[0:16, 0:T], bank["s0"][0:16, 0:T], ACT.Copy).then_inc(act_done, 1)
            act.wait_ge(abs_ready, 1)
            nc.scalar.activation(t3[:, 0:C // 2], t3[:, 0:C // 2], ACT.Exp, scale=-1.0).then_inc(exp_neg, 1)
            act.wait_ge(exp_neg, 1)
            nc.scalar.activation(t3[:, 0:C // 2], t3[:, 0:C // 2], ACT.Ln, bias=one_c).then_inc(ln_ready, 1)
            act.wait_ge(pe_done, 10)
            nc.scalar.activation(t1[:, 0:C // 2], bank["t1"][:, 0:C // 2], ACT.Exp).then_inc(decay_ready, 1)
            nc.scalar.activation(t1[:, C // 2:C], bank["t1"][:, 0:C // 2], ACT.Exp, scale=-1.0).then_inc(decay_ready, 1)
            act.wait_ge(gate_ready, 1)
            nc.scalar.activation(t3[:, :], t3[:, :], ACT.Silu).then_inc(silu_ready, 1)
            act.wait_ge(var_ready, 2)
            nc.scalar.activation(small[:, 1, 0:GH], small[:, 0, 0:GH], ACT.Sqrt).then_inc(std_ready, 1)
            act.wait_ge(var_ready, 3)
            nc.scalar.activation(col[:, 3:4], col[:, 2:3], ACT.Sqrt).then_inc(std_ready, 1)
            act.wait_ge(logit_ready, 1)
            nc.scalar.activation(small[:, 2, :], small[:, 0, :], ACT.Exp, bias=col[:, 10:11],
                                 accum_out=col[:, 11:12]).then_inc(route_ready, 1)
            for e in range(E):
                act.wait_ge(up_done, e + 1)
                if e >= 2:
                    act.wait_ge(act_ready, e - 1)
                nc.scalar.activation(silu_e[e % 2][:, :], ps_s[e % 2][:, 0:I], ACT.Silu).then_inc(silu_done, 1)

        @block.gpsimd
        def _(pool):
            def split(s, slot, c):
                width = KB0 if isinstance(s, int) and s == 0 else KB
                pool.wait_ge(ctx_hi_ready, CC * s + c + 1)
                nc.gpsimd.tensor_tensor(c_lo[slot][:, c, 0:width], raw[slot][:, c, 0:width],
                                        c_hi[slot][:, c, 0:width].bitcast(F32), ALU.subtract)\
                  .then_inc(ctx_lo_ready, 1)

            def period(p, half, parity):
                for q in range(G):
                    for c in CHUNKS_IN[q]:
                        split(p + 2, parity, c)

            for c in range(CC):
                split(0, 0, c)
            for n, (hi, lo, src) in enumerate(((wk_hi, wk_lo, wk_nat), (wv_hi, wv_lo, wv_nat))):
                for c in range(CC):
                    pool.wait_ge(w_hi_ready, CC * n + c + 1)
                    nc.gpsimd.tensor_tensor(lo[:, c, :], src[:, c, :], hi[:, c, :].bitcast(F32),
                                            ALU.subtract).then_inc(w_lo_ready, 1)
            for c in range(CC):
                split(1, 1, c)
            period(0, 0, 0)
            with pool.Fori(0, LOOP_PERIODS) as i:
                period(2 * i + 1, i, 1)
                period(2 * i + 2, i + 1, 0)
            pool.wait_ge(scores_kept, 4)
            nc.gpsimd.affine_select(out=at_sb[:, :, :], in_=at_sb[:, :, :], compare_op=ALU.is_ge, fill=0.0,
                                    base=0, pattern=[[0, GH], [1, T]], channel_multiplier=-1).then_inc(pool_done, 1)

        @block.vector
        def _(dve):
            chained = [0]

            def link(ins):
                chained[0] += 1
                ins.then_inc(dve_chain, 1)
                dve.wait_ge(dve_chain, chained[0])

            def variance(src):
                link(nc.vector.bn_stats(stats[:, :], src))
                link(nc.vector.bn_aggr(col[:, 0:2], stats[:, :]))
                return nc.vector.tensor_scalar(col[:, 2:3], col[:, 1:2], EPS_LN, None, ALU.add)

            def normalise(dst, src):
                link(nc.vector.reciprocal(col[:, 4:5], col[:, 3:4]))
                return nc.vector.tensor_scalar(dst, src, col[:, 0:1], col[:, 4:5], ALU.subtract, ALU.mult)

            def scales(scale, inverse, src, n):
                link(nc.vector.tensor_reduce(scale, src, AX.X, ALU.max, apply_absolute_value=True))
                link(nc.vector.tensor_scalar(scale, scale, 1.0 / QMAX, EPS_Q, ALU.mult, ALU.max))
                link(nc.vector.reciprocal(inverse, scale))

            def rounded(dst, tmp):
                link(nc.vector.tensor_scalar(tmp, tmp, -ROUND, QMAX, ALU.add, ALU.min))
                return nc.vector.tensor_scalar(dst, tmp, -QMAX, None, ALU.max)

            def weight(scale, inverse, w_nat, w_rnd, w_q):
                scales(scale, inverse, w_nat[:, :, :], CC)
                for k in range(CC):
                    ins = nc.vector.tensor_scalar(w_rnd[:, k, :], w_nat[:, k, :], inverse[:, k:k + 1], ROUND,
                                                  ALU.mult, ALU.add)
                link(ins)
                nc.vector.memset(col[:, 9:10], 0.0).then_inc(wq_free, 1)
                return rounded(w_q, w_rnd[:, :, :])

            def keys_lo(s, g):
                width = KB0 if isinstance(s, int) and s == 0 else KB
                dve.wait_ge(k_hi_ready, G * s + g + 1)
                if g >= 2 or not (isinstance(s, int) and s == 0):
                    dve.wait_ge(k_landed[(g - 2) % 4], STACKED * (s + 1) if g >= 2 else STACKED * s)
                nc.vector.scalar_tensor_tensor(out=k_lo[g % 2][:, 0:width], in0=keys_bank(s, g),
                                               scalar=bk_c[:, g:g + 1], in1=k_hi[g % 2][:, 0:width].bitcast(F32),
                                               op0=ALU.add, op1=ALU.subtract).then_inc(k_lo_ready, 1)

            def values(s, t, slot):
                dve.wait_ge(v_projected, tiles_before(s) + t + 1)
                nc.vector.tensor_tensor(v_sb[slot][:, t, :], values_bank(s, t), bv_b[:, :], ALU.add)\
                  .then_inc(v_ready, 1)

            def mask_pair(s, g, j, slot, half):
                width = KB0 if isinstance(s, int) and s == 0 else KB
                n = H * s + HG * g + j
                if j == 0 and g == 0:
                    dve.wait_ge(mask_landed[slot], 16 * (half + 1))
                if isinstance(s, int) and s == 0 and g < 2:
                    pass
                else:
                    if j == 0:
                        gn = tiles_before(s) * G + g * block_tiles(s) if not (isinstance(s, int) and s == 0) else 0
                        if isinstance(s, int) and s == 0:
                            dve.wait_ge(turned, (g - 1) * (KB0 // P))
                        elif g == 0:
                            dve.wait_ge(turned, turned_before(s, g))
                        else:
                            dve.wait_ge(turned, turned_before(s, g))
                dve.wait_ge(scored, n + 2)
                if not (isinstance(n, int) and n == 0):
                    dve.wait_ge(masked, n)
                    if (g, j) == (0, 2) and not (isinstance(s, int) and s == 0):
                        dve.wait_ge(rescale_ready, s)
                    ph = (HG * g + j - 2) % H
                    now, old = (slot, 1 - slot) if (g, j) != (0, 0) else (1 - slot, slot)
                    nc.vector.tensor_tensor(drop[:, ph:ph + 2], neg_max[now][:, ph:ph + 2],
                                            neg_max[old][:, ph:ph + 2], ALU.subtract).then_inc(drop_ready, 1)
                for h in (HG * g + j, HG * g + j + 1):
                    nc.vector.tensor_tensor_reduce(out=prob[:, h % SLOTS, 0:width], in0=ps_s[h % 2][:, 0:width],
                                                   in1=mask_sb[slot][:, 0:width], scale=-1.0,
                                                   scalar=neg_max[1 - slot][:, h:h + 1], op0=ALU.add, op1=ALU.min,
                                                   accum_out=neg_max[slot][:, h:h + 1]).then_inc(masked, 1)

            def turned_before(s, g):
                if g >= 2:
                    return tiles_before(s) * G + (g - 1) * NT
                if isinstance(s, int) and s == 1:
                    return (G + g - 1) * (KB0 // P)
                return tiles_before(s) * G - (1 - g) * NT

            def keep(s, g, t):
                n = tiles_before(s) * G + g * block_tiles(s) + t
                dve.wait_ge(turned, n + 1)
                nc.vector.tensor_copy(probT[:, t, :], ps_t[1][:, :]).then_inc(kept_odd, 1)

            def fold(s, slot):
                dve.wait_ge(group_applied, G * (s + 1))
                dve.wait_ge(prob_ready, H * (s + 1))
                flat = acc[:, :, :].rearrange("p g t -> p (g t)")
                dve.wait_ge(rescale_turned, s + 1)
                nc.vector.tensor_tensor(l_sum[:, :], l_sum[:, :], rescale_w[:, :, 0], ALU.mult).then_inc(scaled, 1)
                nc.vector.tensor_tensor(flat, flat, bank["a"][:, :], ALU.mult).then_inc(scaled, 1)
                dve.wait_ge(scaled, 2 * s + 2)
                nc.vector.tensor_tensor(l_sum[:, :], l_sum[:, :], row_sum[slot][:, :], ALU.add)
                nc.vector.tensor_tensor(flat, flat, bank["o"][:, :], ALU.add).then_inc(folded, 1)

            def wo_step(q):
                scale, inverse = col[:, 12:16], col[:, 16:20]
                if q == 1:
                    dve.wait_ge(wo_landed, 16)
                    scales(scale, inverse, wo_nat[:, :, :], CC)
                elif q == 2:
                    for k in range(CC):
                        ins = nc.vector.tensor_scalar(wo_rnd[:, k, :], wo_nat[:, k, :], inverse[:, k:k + 1], ROUND,
                                                      ALU.mult, ALU.add)
                    link(ins)
                elif q == 3:
                    rounded(wo_q, wo_rnd[:, :, :])
                    for k in range(CC):
                        ins = nc.vector.tensor_copy(wo_scale_w[:, k, :], scale[:, k:k + 1].to_broadcast([P, P]))
                    ins.then_inc(wo_ready, 1)

            def period(p, half, parity, project=True, with_wo=False):
                nt = block_tiles(p)
                for q in range(G):
                    if with_wo:
                        wo_step(q)
                    s, g = (p, q + 1) if q < 3 else (p + 1, 0)
                    slot = parity if q < 3 else 1 - parity
                    mhalf = half if q < 3 else (half if parity == 0 else half + 1)
                    scores = q < 3 or project
                    if scores:
                        mask_pair(s, g, 0, slot, mhalf)
                    elif q == 3:
                        last_drop()
                    if q == 0 and not (isinstance(p, int) and p == 0):
                        fold(p - 1, 1 - parity)
                    keep(p, q, 1)
                    if scores:
                        mask_pair(s, g, 2, slot, mhalf)
                    if project:
                        keys_lo(p + 1, q)
                    if nt > 2:
                        keep(p, q, 3)
                    if project:
                        values(p + 1, q, 1 - parity)

            def last_drop():
                s = NB - 1
                dve.wait_ge(masked, H * NB)
                nc.vector.tensor_tensor(drop[:, H - 2:H], neg_max[s % 2][:, H - 2:H], neg_max[1 - s % 2][:, H - 2:H],
                                        ALU.subtract).then_inc(drop_ready, 1)

            dve.wait_ge(x_landed, 16)
            link(variance(x_sb[:, :]))
            nc.vector.memset(neg_max[1][:, :], BIG).then_inc(init_ready, 1)
            nc.vector.memset(l_sum[:, :], 0.0).then_inc(init_ready, 1)
            nc.vector.memset(acc[:, :, :], 0.0).then_inc(init_ready, 1)
            dve.wait_ge(act_done, 1)
            link(normalise(x_norm[:, :], x_sb[:, :]))
            scales(col[:, 5:6], col[:, 6:7], x_norm[:, :], 1)
            link(nc.vector.tensor_scalar(x_norm[:, :], x_norm[:, :], col[:, 6:7], ROUND, ALU.mult, ALU.add))
            link(rounded(xq[:, :], x_norm[:, :]))
            dve.wait_ge(const_landed, 16)
            nc.vector.tensor_copy(x_scale_w[:, :], col[:, 5:6].to_broadcast([P, P])).then_inc(quant_ready, 1)
            nc.vector.tensor_copy(ident_bf[:, :], ident[:, :]).then_inc(ident_ready, 1)
            dve.wait_ge(wq_landed, 16)
            weight(col[:, 12:16], col[:, 16:20], wq_nat, wq_rnd, wq_q[:, :, :]).then_inc(quant_ready, 1)
            dve.wait_ge(bias_landed, 16 * 4)
            keys_lo(0, 0)
            dve.wait_ge(quant_turned, 1)
            nc.vector.tensor_copy(xqT[:, :, :].rearrange("p c t -> p (c t)"),
                                  bank["t0"][:, :].bitcast(BF16)[:, 0:C]).then_inc(turned_kept, 1)
            nc.vector.tensor_copy(x_scale_b, bank["t1"][:, 0:T])

            def keep_weight(dst, banks):
                nc.vector.tensor_copy(dst[:, 0:2, :].rearrange("p c o -> p (c o)"), bank[banks[0]][:, :].bitcast(BF16))
                return nc.vector.tensor_copy(dst[:, 2:4, :].rearrange("p c o -> p (c o)"),
                                             bank[banks[1]][:, :].bitcast(BF16))

            dve.wait_ge(quant_turned, 2)
            keep_weight(wqT, ("s0", "s1")).then_inc(turned_kept, 1)

            def stack(g, parts):
                dve.wait_ge(k_lo_ready, g + 1)
                for j in range(HG):
                    for r, part in parts:
                        nc.vector.tensor_copy(k_stack[r * D:(r + 1) * D, HG * g + j, 0:KB0],
                                              part[g % 2][j * D:(j + 1) * D, 0:KB0]).then_inc(k_landed[g], 16)

            stack(0, ((1, k_lo),))
            keys_lo(0, 1)
            stack(1, ((1, k_lo),))
            dve.wait_ge(q_made, 1)
            for g in range(G):
                ins = nc.vector.scalar_tensor_tensor(out=q_sb[:, g, :], in0=bank["t0"][:, g * T:(g + 1) * T],
                                                     scalar=col[:, 12 + g:13 + g], in1=x_scale_b, op0=ALU.mult, op1=ALU.mult)
            link(ins)
            for g in range(G):
                ins = nc.vector.tensor_scalar(q_sb[:, g, :], q_sb[:, g, :], bq_c[:, g:g + 1], float(D) ** -0.5,
                                              ALU.add, ALU.mult)
            ins.then_inc(q_ready, 1)
            dve.wait_ge(q_hi_ready, 1)
            nc.vector.tensor_tensor(q_lo[:, :, :], q_sb[:, :, :], q_hi[:, :, :].bitcast(F32), ALU.subtract)\
              .then_inc(q_lo_ready, 1)
            for j in range(HG):
                nc.vector.tensor_copy(heads_of_row(1, j), q_hi[j * D:(j + 1) * D, :, :]).then_inc(q_landed, 16)
            dve.wait_ge(q_lo_ready, 1)
            for j in range(HG):
                nc.vector.tensor_copy(heads_of_row(2, j), q_lo[j * D:(j + 1) * D, :, :]).then_inc(q_landed, 16)
            keys_lo(0, 2)
            stack(2, ((1, k_lo), (2, k_hi)))
            dve.wait_ge(w_lo_ready, 2 * CC)
            for t in range(KB0 // P):
                values(0, t, 0)
            mask_pair(0, 0, 0, 0, 0)
            mask_pair(0, 0, 2, 0, 0)
            keys_lo(0, 3)
            stack(3, ((1, k_lo), (2, k_hi)))

            period(0, 0, 0)
            with dve.Fori(0, LOOP_PERIODS) as i:
                period(2 * i + 1, i, 1)
                period(2 * i + 2, i + 1, 0)
            period(NB - 2, (NB - 2) // 2, (NB - 2) % 2, with_wo=True)
            dve.wait_ge(quant_turned, 3)
            keep_weight(woT, ("k", "v")).then_inc(turned_kept, 1)
            period(NB - 1, (NB - 1) // 2, (NB - 1) % 2, project=False)
            dve.wait_ge(quant_turned, 4)
            nc.vector.tensor_copy(wo_scale_b[:, :], bank["k"][:, :])
            fold(NB - 1, (NB - 1) % 2)

            dve.wait_ge(folded, NB)
            link(nc.vector.reciprocal(col[:, 24:24 + H], l_sum[:, :]))
            dve.wait_ge(pe_done, 1)
            link(nc.vector.tensor_tensor(t0[:, :].rearrange("p (h d) -> p h d", h=H),
                                         bank["t0"][:, :].rearrange("p (h d) -> p h d", h=H),
                                         col[:, 24:24 + H].unsqueeze(2).to_broadcast([P, H, D]), ALU.mult))
            scales(col[:, 5:6], col[:, 6:7], t0[:, :], 1)
            link(nc.vector.tensor_scalar(t0[:, :], t0[:, :], col[:, 6:7], ROUND, ALU.mult, ALU.add))
            rounded(o_q[:, :], t0[:, :]).then_inc(dve_done, 1)
            dve.wait_ge(pe_done, 2)
            nc.vector.tensor_copy(o_qT[:, :, :].rearrange("p c t -> p (c t)"),
                                  bank["t1"][:, :].bitcast(BF16)[:, 0:C]).then_inc(dve_done, 1)
            dve.wait_ge(pe_done, 3)
            link(nc.vector.scalar_tensor_tensor(out=t0[:, :], in0=bank["s0"][:, :], scalar=col[:, 5:6],
                                                in1=wo_scale_b[:, :], op0=ALU.mult, op1=ALU.mult))
            link(nc.vector.tensor_tensor(t0[:, :], t0[:, :], bo_b[:, :], ALU.add))
            link(nc.vector.tensor_tensor(x_sb[:, :], x_sb[:, :], t0[:, :], ALU.add))

            variance(x_sb[:, :]).then_inc(var_ready, 1)
            nc.vector.memset(one_c, 1.0)
            dve.wait_ge(std_ready, 1)
            normalise(t1[:, :], x_sb[:, :]).then_inc(dve_done, 1)
            dve.wait_ge(pe_done, 4)
            nc.vector.tensor_copy(xT[:, :, :].rearrange("p c t -> p (c t)"), bank["t0"][:, :]).then_inc(dve_done, 1)
            dve.wait_ge(pe_done, 7)
            dve.wait_ge(tail_landed, 16 * 7)
            HC = C // 2
            link(nc.vector.tensor_tensor(t0[:, 0:HC], bank["s1"][:, 0:HC], bkg2_b[:, :], ALU.add))
            nc.vector.scalar_tensor_tensor(out=t3[:, 0:HC], in0=t0[:, 0:HC], scalar=-1.0, in1=t0[:, 0:HC],
                                           op0=ALU.mult, op1=ALU.max).then_inc(abs_ready, 1)
            dve.wait_ge(abs_ready, 1)
            link(nc.vector.tensor_scalar(t0[:, 0:HC], t0[:, 0:HC], 0.0, 1.0 / 16.0, ALU.min, ALU.mult))
            dve.wait_ge(ln_ready, 1)
            nc.vector.scalar_tensor_tensor(out=t0[:, 0:HC], in0=t3[:, 0:HC], scalar=-1.0 / 16.0, in1=t0[:, 0:HC],
                                           op0=ALU.mult, op1=ALU.add).then_inc(dve_done, 1)
            dve.wait_ge(decay_ready, 2)
            nc.vector.tensor_tensor(t2[:, 0:HC], bank["k"][:, 0:HC], t1[:, 0:HC], ALU.mult)
            nc.vector.scalar_tensor_tensor(out=t2[:, HC:C], in0=bank["v"][:, 0:HC], scalar=float(GV) ** -0.5,
                                           in1=t1[:, HC:C], op0=ALU.mult, op1=ALU.mult).then_inc(dve_done, 1)
            dve.wait_ge(pe_done, 9)
            nc.vector.tensor_tensor(t3[:, :], bank["a"][:, :], bg_b[:, :], ALU.add).then_inc(gate_ready, 1)
            nc.vector.tensor_copy(v_gla[:, :], bank["o"][:, :]).then_inc(dve_done, 1)
            dve.wait_ge(pe_done, 11)
            for r, at in enumerate(("s0", "s1", "t0", "t1")):
                dst = at_sb[:, :, :].rearrange("p (m r) t -> p m r t", r=4)[:, :, r, :]
                nc.vector.tensor_copy(dst, bank[at][:, 0:GKT * T].rearrange("p (m t) -> p m t", m=GKT))\
                  .then_inc(scores_kept, 1)
            dve.wait_ge(pe_done, 12)
            heads = lambda t: t[:, :].rearrange("p (h d) -> p h d", h=GH)
            wide = lambda c: c.unsqueeze(2).to_broadcast([P, GH, GV])
            link(nc.vector.tensor_reduce(small[:, 0, 0:GH], heads(bank["k"]), AX.X, ALU.add))
            link(nc.vector.tensor_scalar(small[:, 0, 0:GH], small[:, 0, 0:GH], 1.0 / GV, None, ALU.mult))
            link(nc.vector.tensor_tensor(heads(t0), heads(bank["k"]), wide(small[:, 0, 0:GH]), ALU.subtract))
            link(nc.vector.tensor_tensor(t1[:, :], t0[:, :], t0[:, :], ALU.mult))
            link(nc.vector.tensor_reduce(small[:, 0, 0:GH], heads(t1), AX.X, ALU.add))
            nc.vector.tensor_scalar(small[:, 0, 0:GH], small[:, 0, 0:GH], 1.0 / GV, EPS_LN, ALU.mult, ALU.add)\
              .then_inc(var_ready, 1)
            dve.wait_ge(std_ready, 2)
            dve.wait_ge(silu_ready, 1)
            link(nc.vector.reciprocal(small[:, 2, 0:GH], small[:, 1, 0:GH]))
            link(nc.vector.tensor_tensor(t0[:, :], t0[:, :], t3[:, :], ALU.mult))
            nc.vector.tensor_tensor(heads(t0), heads(t0), wide(small[:, 2, 0:GH]), ALU.mult).then_inc(dve_done, 1)
            dve.wait_ge(pe_done, 13)
            nc.vector.tensor_copy(xT[:, :, :].rearrange("p c t -> p (c t)"), bank["v"][:, :]).then_inc(dve_done, 1)
            dve.wait_ge(pe_done, 14)
            link(nc.vector.tensor_tensor(x_sb[:, :], x_sb[:, :], bank["o"][:, :], ALU.add))

            variance(x_sb[:, :]).then_inc(var_ready, 1)
            dve.wait_ge(std_ready, 3)
            normalise(t1[:, :], x_sb[:, :]).then_inc(dve_done, 1)
            dve.wait_ge(pe_done, 15)
            nc.vector.tensor_copy(xT[:, :, :].rearrange("p c t -> p (c t)"), bank["t0"][:, :]).then_inc(dve_done, 1)
            dve.wait_ge(pe_done, 16)
            link(nc.vector.tensor_copy(small[:, 0, :], bank["t1"][:, 0:E]))
            nc.vector.tensor_reduce(col[:, 10:11], small[:, 0, :], AX.X, ALU.max, negate=True).then_inc(logit_ready, 1)
            dve.wait_ge(route_ready, 1)
            link(nc.vector.reciprocal(col[:, 12:13], col[:, 11:12]))
            link(nc.vector.tensor_scalar(small[:, 2, :], small[:, 2, :], col[:, 12:13], None, ALU.mult))
            link(nc.vector.max(small[:, 3, 0:8], small[:, 2, :]))
            link(nc.vector.max_index(top_ids[:, :], small[:, 3, 0:8], small[:, 2, :]))
            link(nc.vector.tensor_copy(small[:, 4, 0:8], top_ids[:, :]))
            link(nc.vector.tensor_tensor(col[:, 13:14], small[:, 3, 0:1], small[:, 3, 1:2], ALU.add))
            link(nc.vector.tensor_scalar(col[:, 13:14], col[:, 13:14], 1e-20, None, ALU.add))
            link(nc.vector.reciprocal(col[:, 14:15], col[:, 13:14]))
            link(nc.vector.tensor_scalar(small[:, 3, 0:2], small[:, 3, 0:2], col[:, 14:15], None, ALU.mult))
            for n in range(2):
                ins = nc.vector.tensor_scalar(small[:, 5 + n, :], ids_sb[:, :], small[:, 4, n:n + 1],
                                              small[:, 3, n:n + 1], ALU.is_equal, ALU.mult)
            link(ins)
            link(nc.vector.tensor_tensor(small[:, 7, :], small[:, 5, :], small[:, 6, :], ALU.add))

            def keep_act(e):
                dve.wait_ge(act_turned, e + 1)
                if e >= 2:
                    dve.wait_ge(down_done, e - 1)
                nc.vector.tensor_copy(act_eT[e % 2][:, :, :].rearrange("p c t -> p (c t)"),
                                      bank["k" if e % 2 == 0 else "v"][:, 0:I]).then_inc(act_kept, 1)

            for e in range(E + 1):
                if e < E:
                    dve.wait_ge(silu_done, e + 1)
                    if e >= 2:
                        dve.wait_ge(act_turned, e - 1)
                    nc.vector.scalar_tensor_tensor(out=act_e[e % 2][:, :], in0=silu_e[e % 2][:, :],
                                                   scalar=small[:, 7, e:e + 1], in1=ps_s[e % 2][:, I:2 * I],
                                                   op0=ALU.mult, op1=ALU.mult).then_inc(act_ready, 1)
                if e >= 1:
                    keep_act(e - 1)
            dve.wait_ge(down_done, E)
            nc.vector.tensor_copy(t0[:, :], bank["a"][:, :]).then_inc(out_ready, 1)


def kernel(**inputs):
    import numpy as np
    import concourse.bacc as bacc
    from concourse import mybir as _mybir
    from concourse.bass_utils import run_bass_kernel_spmd as run

    a = {k: np.asarray(v) for k, v in inputs.items()}
    ctx = a["ctx_2048"][0]
    chunks = lambda w: w.reshape(CC, P, -1).transpose(1, 0, 2)
    arrays = {
        "x": a["x"][0],
        "ctx_first": chunks(ctx[:KB0].T),
        "ctx_rest": ctx[KB0:].reshape(NB - 1, KB, CC, P).transpose(0, 3, 2, 1),
        "mask": a["mask_BxSxS2_ff0"][0],
        "wq": chunks(a["L0_xattn_wq"]),
        "bq": a["L0_xattn_bq"].reshape(G, P).T,
        "wkT": chunks(a["L0_xattn_wk"].T),
        "bk": a["L0_xattn_bk"].reshape(G, P).T,
        "wvT": chunks(a["L0_xattn_wv"].T),
        "bv": a["L0_xattn_bv"],
        "wo": chunks(a["L0_xattn_wo"]),
        "bo": a["L0_xattn_bo"],
        "g_wq": a["L0_attn_Wq"],
        "g_wk": a["L0_attn_Wk"],
        "g_wkg1": chunks(a["L0_attn_Wkg1"]),
        "g_wkg2": a["L0_attn_Wkg2"],
        "g_bkg2": a["L0_attn_bkg2"],
        "g_wv": a["L0_attn_Wv"],
        "g_wg": a["L0_attn_Wg"],
        "g_bg": a["L0_attn_bg"],
        "g_wo": a["L0_attn_Wo"],
        "gateT": chunks(a["L0_ffn_gate_w"].T),
        "wg": a["L0_ffn_wg"],
        "wu": a["L0_ffn_wu"],
        "wd": a["L0_ffn_wd"],
        "eye": np.eye(P, dtype=np.float32),
        "upper": np.triu(np.ones((P, P), np.float32)),
        "expert_ids": np.arange(E, dtype=np.float32),
    }
    arrays = {k: np.ascontiguousarray(v) for k, v in arrays.items()}
    nc = bacc.Bacc("TRN2", target_bir_lowering=False, num_devices=1)
    aps = {k: nc.dram_tensor(f"in_{k}", v.shape, _mybir.dt.from_np(v.dtype), kind="ExternalInput").ap()
           for k, v in arrays.items()}
    out = nc.dram_tensor("out_y", (T, C), _mybir.dt.float32, kind="ExternalOutput").ap()
    perceiver_kernel(nc, **aps, out=out)
    r = run(nc, [{f"in_{k}": v for k, v in arrays.items()}], core_ids=[0])
    return r.results[0]["out_y"].reshape(1, T, C)
```

```python
from contextlib import ExitStack

import concourse.bass as bass
from concourse import mybir

ALU = mybir.AluOpType
ACT = mybir.ActivationFunctionType
AX = mybir.AxisListType
F32 = mybir.dt.float32
F32R = mybir.dt.float32r
BF16 = mybir.dt.bfloat16
U32 = mybir.dt.uint32

P = 128
T = 128
C = 512
CC = C // P
L = 12544
H = 16
D = C // H
G = 4
HG = H // G
KB = 512
KB0 = 256
NB = (L - KB0) // KB + 1
NT = KB // P
LOOP_PERIODS = (NB - 3) // 2
SLOTS = 8

GH = 8
GK = C // 2 // GH
GV = C // GH
GKT = C // 2 // P
E = 16
I = 256
EPS_LN = 1e-5
EPS_Q = 1e-8
QMAX = 127.0
ROUND = 12582912.0
BIG = 3.0e38
EXPERT_SLOTS = 7
CHUNKS_IN = ((), (0, 1), (2,), (3,))


def block_tiles(s):
    return KB0 // P if isinstance(s, int) and s == 0 else NT


def tiles_before(s):
    return 0 if isinstance(s, int) and s == 0 else NT * s - (NT - KB0 // P)


def perceiver_kernel(nc, x, ctx_first, ctx_rest, mask, wq, bq, wkT, bk, wvT, bv, wo, bo,
                     g_wq, g_wk, g_wkg1, g_wkg2, g_bkg2, g_wv, g_wg, g_bg, g_wo,
                     gateT, wg, wu, wd, eye, upper, expert_ids, out):
    ctx = ExitStack()
    with ctx:
        def sb(name, shape, dt=F32, where=ctx):
            return where.enter_context(nc.sbuf_tensor(name, shape, dt))

        def sem(name):
            return ctx.enter_context(nc.semaphore(name))

        x_sb = sb("x_sb", [P, C])
        ident = sb("ident", [P, P])
        ident_bf = sb("ident_bf", [P, P], BF16)
        woT = sb("woT", [P, CC, C], BF16)
        wo_scale_b = sb("wo_scale_b", [P, C])
        bo_b = sb("bo_b", [P, C])
        acc = sb("acc", [P, G, T])
        l_sum = sb("l_sum", [P, H])
        col = sb("col", [P, 64])
        stats = sb("stats", [P, 6])

        att = ExitStack()
        wk_hi = sb("wk_hi", [P, CC, C], F32R, att)
        wk_lo = sb("wk_lo", [P, CC, C], F32R, att)
        wv_hi = sb("wv_hi", [P, CC, C], F32R, att)
        wv_lo = sb("wv_lo", [P, CC, C], F32R, att)
        c_hi = [sb(f"c_hi{i}", [P, CC, KB], F32R, att) for i in range(2)]
        c_lo = [sb(f"c_lo{i}", [P, CC, KB], F32R, att) for i in range(2)]
        raw = [sb(f"raw{i}", [P, CC, KB], F32, att) for i in range(2)]
        v_sb = [sb(f"v_sb{i}", [P, NT, C], F32, att) for i in range(2)]
        k_stack = sb("k_stack", [96, H, KB], F32R, att)
        q_stack = sb("q_stack", [96, HG, G, T], F32R, att)
        k_hi = [sb(f"k_hi{i}", [P, KB], F32R, att) for i in range(2)]
        k_lo = [sb(f"k_lo{i}", [P, KB], F32R, att) for i in range(2)]
        mask_sb = [sb(f"mask_sb{i}", [P, KB], F32, att) for i in range(2)]
        neg_max = [sb(f"neg_max{i}", [P, H], F32, att) for i in range(2)]
        row_sum = [sb(f"row_sum{i}", [P, H], F32, att) for i in range(2)]
        drop = sb("drop", [P, H], F32, att)
        rescale_w = sb("rescale_w", [P, H, D], F32, att)
        bv_b = sb("bv_b", [P, C], F32, att)
        bq_c = sb("bq_c", [P, G], F32, att)
        bk_c = sb("bk_c", [P, G], F32, att)

        wq_nat = raw[1]
        wq_rnd = v_sb[1]
        wk_nat = v_sb[0]
        att_end = ExitStack()
        wv_nat = sb("wv_nat", [P, CC, C], F32, att_end)
        wqT = sb("wqT", [P, CC, C], BF16, att_end)
        wq_q = sb("wq_q", [P, CC, C], BF16, att_end)
        xq = sb("xq", [P, C], BF16, att_end)
        xqT = sb("xqT", [P, CC, T], BF16, att_end)
        x_norm = sb("x_norm", [P, C], F32, att_end)
        x_scale_w = sb("x_scale_w", [P, P], F32, att_end)
        q_sb = sb("q_sb", [P, G, T], F32, att_end)
        x_scale_b = x_norm[:, 0:T]
        q_hi = sb("q_hi", [P, G, T], F32R, att_end)
        q_lo = sb("q_lo", [P, G, T], F32R, att_end)
        att_end.close()
        wo_nat = raw[0]
        wo_rnd = raw[1]
        wo_q = raw[0][:, 0:2, :].bitcast(BF16).rearrange("p a b -> p (a b)").rearrange("p (c i) -> p c i", c=CC)
        wo_scale_w = raw[0][:, 2, :].rearrange("p (c t) -> p c t", c=CC)
        prob = sb("prob", [P, SLOTS, KB], F32, att)
        probT = sb("probT", [P, NT, HG * T], F32, att)
        att.close()

        w_gq = sb("w_gq", [P, CC, C // 2])
        w_gk = sb("w_gk", [P, CC, C // 2])
        w_gv = sb("w_gv", [P, CC, C])
        w_gg = sb("w_gg", [P, CC, C])
        w_go = sb("w_go", [P, CC, C])
        as_it_comes = ExitStack()
        experts_at = [sb(f"expert{i}", [P, 3, 1024], F32, as_it_comes) for i in range(EXPERT_SLOTS)]
        as_it_comes.close()
        experts_lo = [sb(f"expert_lo{i}", [P, 3, 1024], F32R) for i in range(EXPERT_SLOTS)]
        w_kg1 = sb("w_kg1", [P, CC, 16])
        w_kg2 = sb("w_kg2", [16, C // 2])
        bkg2_b = sb("bkg2_b", [P, C // 2])
        bg_b = sb("bg_b", [P, C])
        upper_sb = sb("upper_sb", [P, P])
        gate_sb = sb("gate_sb", [P, CC, E])
        ids_sb = sb("ids_sb", [P, E])
        t0 = sb("t0", [P, C])
        t1 = sb("t1", [P, C])
        t2 = sb("t2", [P, C])
        t3 = sb("t3", [P, C])
        v_gla = sb("v_gla", [P, C])
        xT = sb("xT", [P, CC, T])
        o_q = sb("o_q", [P, C], BF16)
        o_qT = sb("o_qT", [P, CC, T], BF16)
        small = sb("small", [P, 8, E])
        top_ids = sb("top_ids", [P, 8], U32)
        at_sb = sb("at_sb", [P, GH, T])
        act_e = [sb(f"act_e{i}", [P, I]) for i in range(2)]
        silu_e = [sb(f"silu_e{i}", [P, I]) for i in range(2)]
        act_hiT = [sb(f"act_hiT{i}", [P, I // P, T], F32R) for i in range(2)]
        act_loT = [sb(f"act_loT{i}", [P, I // P, T], F32R) for i in range(2)]
        x_hiT = sb("x_hiT", [P, CC, T], F32R)
        x_loT = sb("x_loT", [P, CC, T], F32R)
        up_hi = [sb(f"up_hi{i}", [P, 2, 1024], F32R) for i in range(3)]
        down_hi = [sb(f"down_hi{i}", [P, 1024], F32R) for i in range(3)]

        names = ["s0", "s1", "t0", "t1", "k", "v", "o", "a"]
        bank = {n: ctx.enter_context(nc.psum_tensor(f"bank_{n}", [P, 512], F32)) for n in names}
        ps_s = [bank["s0"], bank["s1"]]
        ps_t = [bank["t0"], bank["t1"]]

        x_landed = sem("x_landed")
        wq_landed = sem("wq_landed")
        wo_landed = sem("wo_landed")
        const_landed = sem("const_landed")
        bias_landed = sem("bias_landed")
        wk_landed = sem("wk_landed")
        wv_landed = sem("wv_landed")
        w_hi_ready = sem("w_hi_ready")
        w_lo_ready = sem("w_lo_ready")
        ctx_landed = [sem(f"ctx_landed{i}") for i in range(2)]
        mask_landed = [sem(f"mask_landed{i}") for i in range(2)]
        ctx_hi_ready = sem("ctx_hi_ready")
        ctx_lo_ready = sem("ctx_lo_ready")
        ident_ready = sem("ident_ready")
        quant_ready = sem("quant_ready")
        quant_turned = sem("quant_turned")
        turned_kept = sem("turned_kept")
        wo_ready = sem("wo_ready")
        wo_scale_ready = sem("wo_scale_ready")
        wo_scale_turned = sem("wo_scale_turned")
        wo_scale_kept = sem("wo_scale_kept")
        wo_kept = sem("wo_kept")
        wq_free = sem("wq_free")
        q_made = sem("q_made")
        q_ready = sem("q_ready")
        q_hi_ready = sem("q_hi_ready")
        q_lo_ready = sem("q_lo_ready")
        q_landed = sem("q_landed")
        init_ready = sem("init_ready")

        k_projected = sem("k_projected")
        v_projected = sem("v_projected")
        k_hi_ready = sem("k_hi_ready")
        k_lo_ready = sem("k_lo_ready")
        k_landed = [sem(f"k_landed{g}") for g in range(G)]
        v_ready = sem("v_ready")
        scored = sem("scored")
        masked = sem("masked")
        drop_ready = sem("drop_ready")
        prob_ready = sem("prob_ready")
        turned = sem("turned")
        kept_even = sem("kept_even")
        kept_odd = sem("kept_odd")
        group_applied = sem("group_applied")
        rescale_ready = sem("rescale_ready")
        rescale_turned = sem("rescale_turned")
        scaled = sem("scaled")
        folded = sem("folded")

        dve_chain = sem("dve_chain")
        pe_done = sem("pe_done")
        act_done = sem("act_done")
        pool_done = sem("pool_done")
        dve_done = sem("dve_done")
        gla_landed = sem("gla_landed")
        tail_landed = sem("tail_landed")
        expert_landed = [sem(f"expert_landed{i}") for i in range(EXPERT_SLOTS)]
        up_done = sem("up_done")
        silu_done = sem("silu_done")
        act_ready = sem("act_ready")
        act_turned = sem("act_turned")
        act_hi_ready = sem("act_hi_ready")
        act_kept = sem("act_kept")
        up_hi_ready = sem("up_hi_ready")
        up_lo_ready = sem("up_lo_ready")
        down_hi_ready = sem("down_hi_ready")
        down_lo_ready = sem("down_lo_ready")
        x_hi_ready = sem("x_hi_ready")
        down_done = sem("down_done")
        out_ready = sem("out_ready")
        var_ready = sem("var_ready")
        std_ready = sem("std_ready")
        abs_ready = sem("abs_ready")
        exp_neg = sem("exp_neg")
        ln_ready = sem("ln_ready")
        decay_ready = sem("decay_ready")
        gate_ready = sem("gate_ready")
        silu_ready = sem("silu_ready")
        scores_kept = sem("scores_kept")
        logit_ready = sem("logit_ready")
        route_ready = sem("route_ready")
        one_c = col[:, 50:51]
        out_landed = sem("out_landed")

        STACKED = 3 * 16

        def keys_bank(s, g):
            if isinstance(s, int) and s == 0:
                return bank[("k", "v", "o", "a")[g]][:, 0:KB0]
            return bank["k"][:, :]

        def score_bank(s, h):
            if isinstance(s, int) and s == NB - 1 and h >= HG and h % HG >= 2:
                return bank[("k", "v")[h % 2]]
            return ps_s[h % 2]

        def values_bank(s, t):
            if isinstance(s, int) and s == 0:
                return bank[("v", "t1")[t]][:, :]
            return bank["v"][:, :]

        block = ctx.enter_context(nc.Block())

        @block.sync
        def _(sp):
            def load_ctx(at, parity):
                if at is None:
                    sp.dma_start(raw[0][:, :, 0:KB0], ctx_first).then_inc(ctx_landed[0], 16)
                else:
                    sp.dma_start(raw[parity][:, :, :], ctx_rest[at]).then_inc(ctx_landed[parity], 16)

            def load_mask(at, parity):
                if isinstance(at, int) and at == 0:
                    sp.dma_start(mask_sb[0][:, 0:KB0], mask[:, 0:KB0]).then_inc(mask_landed[0], 16)
                else:
                    sp.dma_start(mask_sb[parity][:, :], mask[:, bass.ds(at, KB)])\
                      .then_inc(mask_landed[parity], 16)

            def stack_keys(g, width, made):
                sp.wait_ge(k_hi_ready, made)
                sp.wait_ge(k_lo_ready, made)
                for r, part in enumerate((k_hi, k_lo, k_hi)):
                    sp.dma_start(k_stack[r * D:(r + 1) * D, HG * g:HG * (g + 1), 0:width].bitcast(F32),
                                 part[g % 2][:, 0:width].bitcast(F32))\
                      .then_inc(k_landed[g], 16)

            def period(p, half, parity, load=True, project=True):
                value = sp.snap if not isinstance(p, int) else int
                split_before = value(CC * (p + 2))
                block_at = value(p + 2)
                mask_at = value(KB * (p + 1) + KB0)
                masks_before = value(H * (p + 1))
                keys_made = [value(G * (p + 1) + q + 1) for q in range(G)]
                for q in range(G):
                    if q == 3 and load:
                        sp.wait_ge(ctx_lo_ready, split_before)
                        sp.wait_ge(ctx_hi_ready, split_before)
                        load_ctx(block_at, 1 - parity)
                    if project:
                        stack_keys(q, KB, keys_made[q])
                    if q == 3 and project and not (isinstance(p, int) and p + 2 >= NB):
                        sp.wait_ge(masked, masks_before)
                        load_mask(mask_at, parity)

            sp.dma_start(x_sb[:, :], x).then_inc(x_landed, 16)
            load_ctx(None, 0)
            sp.dma_start(wk_nat[:, :, :], wkT).then_inc(wk_landed, 16)
            sp.dma_start(raw[1][:, :, :], wq).then_inc(wq_landed, 16)
            sp.dma_start(ident[:, :], eye).then_inc(const_landed, 16)
            sp.dma_start(wv_nat[:, :, :], wvT).then_inc(wv_landed, 16)
            for where, what in ((bq_c[:, :], bq), (bk_c[:, :], bk), (bv_b[:, :], bv.partition_broadcast(P)),
                                (bo_b[:, :], bo.partition_broadcast(P))):
                sp.dma_start(where, what).then_inc(bias_landed, 16)
            load_mask(0, 0)
            load_mask(KB0, 1)
            sp.wait_ge(wq_free, 1)
            load_ctx(0, 1)
            for g in range(2):
                stack_keys(g, KB0, g + 1)
            for r, part in enumerate((q_hi, q_hi, q_lo)):
                sp.wait_ge(q_hi_ready if r < 2 else q_lo_ready, 1)
                sp.dma_start(q_stack[r * D:(r + 1) * D, :, :, :].bitcast(F32), part[:, :, :].bitcast(F32))\
                  .then_inc(q_landed, 16)
            for g in range(2, G):
                stack_keys(g, KB0, g + 1)
            sp.wait_ge(ctx_lo_ready, CC)
            sp.wait_ge(ctx_hi_ready, CC)
            load_ctx(1, 0)

            period(0, 0, 0)
            with sp.Fori(0, LOOP_PERIODS - 1) as i:
                period(2 * i + 1, i, 1)
                period(2 * i + 2, i + 1, 0)
            period(NB - 4, (NB - 4) // 2, (NB - 4) % 2)
            period(NB - 3, (NB - 3) // 2, (NB - 3) % 2, load=False)
            sp.wait_ge(ctx_hi_ready, CC * NB)
            sp.wait_ge(ctx_lo_ready, CC * NB)
            sp.dma_start(wo_nat[:, :, :], wo).then_inc(wo_landed, 16)
            period(NB - 2, (NB - 2) // 2, (NB - 2) % 2, load=False)

            sp.wait_ge(k_projected, G * NB)
            sp.wait_ge(v_projected, tiles_before(NB))
            for where, what in ((w_gv, g_wv), (w_gg, g_wg), (w_go, g_wo), (w_gq, g_wq), (w_gk, g_wk)):
                sp.dma_start(where[:, :, :], what.rearrange("(c p) n -> p c n", p=P)).then_inc(gla_landed, 16)

            def load_expert(e):
                at = experts_at[e % EXPERT_SLOTS]
                for n, w in enumerate((wg, wu, wd)):
                    sp.dma_start(at[:, n, :].rearrange("p (c i) -> p c i", c=4 if n < 2 else 2),
                                 w[e].rearrange("(c p) i -> p c i", p=P))\
                      .then_inc(expert_landed[e % EXPERT_SLOTS], 16)

            for e in range(2):
                load_expert(e)
            sp.wait_ge(quant_turned, 3)
            for e in range(2, 4):
                load_expert(e)
            sp.wait_ge(folded, NB)
            sp.wait_ge(kept_even, tiles_before(NB) * G // 2)
            for where, what in ((w_kg1[:, :, :], g_wkg1), (w_kg2[:, :], g_wkg2),
                                (bkg2_b[:, :], g_bkg2.partition_broadcast(P)),
                                (bg_b[:, :], g_bg.partition_broadcast(P)), (upper_sb[:, :], upper),
                                (gate_sb[:, :, :], gateT), (ids_sb[:, :], expert_ids.partition_broadcast(P))):
                sp.dma_start(where, what).then_inc(tail_landed, 16)
            for e in range(4, EXPERT_SLOTS):
                load_expert(e)
            for e in range(EXPERT_SLOTS, E):
                sp.wait_ge(down_done, e - EXPERT_SLOTS + 1)
                load_expert(e)
            sp.wait_ge(out_ready, 1)
            sp.dma_start(out, t0[:, :]).then_inc(out_landed, 16)
            sp.wait_ge(out_landed, 16)

        @block.tensor
        def _(pe):
            def project_keys(s, g, part):
                width = KB0 if isinstance(s, int) and s == 0 else KB
                slot = project_slot[0]
                if part == 0:
                    if g == 0:
                        pe.wait_ge(ctx_hi_ready, CC * (s + 1))
                        pe.wait_ge(ctx_lo_ready, CC * (s + 1))
                    if isinstance(s, int) and s == 1 and g == 0:
                        pe.wait_ge(k_lo_ready, 1)
                    elif not (isinstance(s, int) and s == 0):
                        pe.wait_ge(k_lo_ready, G * s + g)
                steps = [(c, a, b) for c in range(CC)
                         for a, b in ((wk_hi, c_hi[slot]), (wk_hi, c_lo[slot]), (wk_lo, c_hi[slot]))]
                for n in range(part * 6, part * 6 + 6):
                    c, a, b = steps[n]
                    mm = nc.tensor.matmul(keys_bank(s, g), a[:, c, g * P:(g + 1) * P],
                                          b[:, c, 0:width], start=(n == 0), stop=(n == 11))
                if part == 1:
                    mm.then_inc(k_projected, 1)

            def project_values(s, t, part):
                slot = project_slot[0]
                if part == 0 and not (isinstance(s, int) and s == 0):
                    pe.wait_ge(v_ready, tiles_before(s) + t)
                steps = [(c, a, b) for c in range(CC)
                         for a, b in ((c_hi[slot], wv_hi), (c_hi[slot], wv_lo), (c_lo[slot], wv_hi))]
                for n in range(part * 6, part * 6 + 6):
                    c, a, b = steps[n]
                    mm = nc.tensor.matmul(values_bank(s, t), a[:, c, t * P:(t + 1) * P], b[:, c, :],
                                          start=(n == 0), stop=(n == 11))
                if part == 1:
                    mm.then_inc(v_projected, 1)

            def score_pair(s, g, j):
                width = KB0 if isinstance(s, int) and s == 0 else KB
                n = H * s + HG * g + j
                if isinstance(s, int) and s == NB - 1 and (g, j) >= (1, 2):
                    if (g, j) == (1, 2):
                        pe.wait_ge(wo_kept, 2)
                    else:
                        pe.wait_ge(masked, n - 2)
                elif not (isinstance(n, int) and n == 0):
                    pe.wait_ge(masked, n)
                if j == 0:
                    pe.wait_ge(k_landed[g], STACKED * (s + 1))
                for h in (j, j + 1):
                    nc.tensor.matmul(score_bank(s, HG * g + h)[:, 0:width], q_stack[:, h, g, :],
                                     k_stack[:, HG * g + h, 0:width], start=True, stop=True).then_inc(scored, 1)

            def turn(s, g, t):
                if t == 0:
                    pe.wait_ge(prob_ready, H * s + HG * (g + 1))
                if not (isinstance(s, int) and s == 0 and g == 0 and t < 2):
                    kept_before = tiles_before(s) * (G // 2) + (g * block_tiles(s) + t - t % 2) // 2
                    pe.wait_ge(kept_even if t % 2 == 0 else kept_odd, kept_before)
                if isinstance(s, int) and s == 0 and g == 0 and t == 1:
                    pe.wait_ge(v_ready, KB0 // P)
                for j in range(HG):
                    tr = nc.tensor.transpose(ps_t[t % 2][:, j * T:(j + 1) * T],
                                             prob[:, (HG * g + j) % SLOTS, t * P:(t + 1) * P], ident[:, :])
                tr.then_inc(turned, 1)

            def apply(s, g, t, slot):
                n = tiles_before(s) * (G // 2) + (g * block_tiles(s) + t - t % 2) // 2
                pe.wait_ge(kept_even if t % 2 == 0 else kept_odd, n + 1)
                if t == 0 and g == 0:
                    pe.wait_ge(v_ready, tiles_before(s) + block_tiles(s))
                    if isinstance(s, int) and s == 0:
                        pe.wait_ge(k_lo_ready, G - 1)
                    else:
                        pe.wait_ge(folded, s)
                for j in range(HG):
                    h = HG * g + j
                    mm = nc.tensor.matmul(bank["o"][j * D:(j + 1) * D, g * T:(g + 1) * T],
                                          v_sb[slot][:, t, h * D:(h + 1) * D], probT[:, t, j * T:(j + 1) * T],
                                          start=(t == 0), stop=(t == block_tiles(s) - 1),
                                          tile_position=(0, j * D))
                if t == block_tiles(s) - 1:
                    mm.then_inc(group_applied, 1)

            def rescale_turn(p):
                pe.wait_ge(rescale_ready, p + 1)
                for g in range(G):
                    tr = nc.tensor.transpose(bank["a"][:, g * T:(g + 1) * T],
                                             rescale_w[:, HG * g:HG * (g + 1), :].rearrange("p h d -> p (h d)"),
                                             ident[:, :])
                tr.then_inc(rescale_turned, 1)

            def last_period(parity):
                p = NB - 1
                score_pair(p, 1, 0)
                for q in range(G):
                    turn(p, q, 0)
                    turn(p, q, 1)
                    if q == 0:
                        score_pair(p, 1, 2)
                    if q + 2 < G:
                        score_pair(p, q + 2, 0)
                    turn(p, q, 2)
                    turn(p, q, 3)
                    if q + 2 < G:
                        score_pair(p, q + 2, 2)
                    if q == G - 1:
                        rescale_turn(p)
                    for t in range(NT):
                        apply(p, q, t, parity)

            def period(p, parity, with_wo=False):
                project_slot[0] = (parity + 1) % 2
                nt = block_tiles(p)
                for q in range(G):
                    s, g = (p, q + 1) if q < 3 else (p + 1, 0)
                    score_pair(s, g, 0)
                    project_keys(p + 1, q, 0)
                    turn(p, q, 0)
                    turn(p, q, 1)
                    project_keys(p + 1, q, 1)
                    score_pair(s, g, 2)
                    project_values(p + 1, q, 0)
                    if q == 3 and with_wo:
                        pe.wait_ge(wo_scale_ready, 1)
                        pe.wait_ge(folded, p)
                        for k in range(CC):
                            tr = nc.tensor.transpose(bank["a"][:, k * P:(k + 1) * P], wo_scale_w[:, k, :], ident[:, :])
                        tr.then_inc(wo_scale_turned, 1)
                    if nt > 2:
                        turn(p, q, 2)
                        turn(p, q, 3)
                    project_values(p + 1, q, 1)
                    for t in range(nt):
                        apply(p, q, t, parity)
                if with_wo:
                    pe.wait_ge(wo_scale_kept, 1)
                rescale_turn(p)

            project_slot = [0]

            def turn_weight(w_q, banks):
                for c in range(CC):
                    view = bank[banks[c // 2]][:, :].bitcast(BF16)
                    for k in range(CC):
                        at = (c % 2) * C + k * P
                        tr = nc.tensor.transpose(view[:, at:at + P], w_q[:, k, c * P:(c + 1) * P], ident_bf[:, :])
                return tr

            pe.wait_ge(w_hi_ready, CC)
            pe.wait_ge(w_lo_ready, CC)
            for g in range(2):
                project_keys(0, g, 0)
                project_keys(0, g, 1)
            pe.wait_ge(ident_ready, 1)
            pe.wait_ge(quant_ready, 1)
            xqT_ps = bank["t0"][:, :].bitcast(BF16)
            for c in range(CC):
                nc.tensor.transpose(xqT_ps[:, c * T:(c + 1) * T], xq[:, c * P:(c + 1) * P], ident_bf[:, :])
            nc.tensor.transpose(bank["t1"][:, 0:T], x_scale_w[:, :], ident[:, :]).then_inc(quant_turned, 1)
            pe.wait_ge(quant_ready, 2)
            turn_weight(wq_q, ("s0", "s1")).then_inc(quant_turned, 1)
            project_keys(0, 2, 0)
            project_keys(0, 2, 1)
            pe.wait_ge(turned_kept, 2)
            for g in range(G):
                for c in range(CC):
                    mm = nc.tensor.matmul(bank["t0"][:, g * T:(g + 1) * T], wqT[:, c, g * P:(g + 1) * P],
                                          xqT[:, c, :], start=(c == 0), stop=(c == CC - 1))
            mm.then_inc(q_made, 1)
            project_keys(0, 3, 0)
            project_keys(0, 3, 1)
            pe.wait_ge(w_hi_ready, 2 * CC)
            pe.wait_ge(w_lo_ready, 2 * CC)
            pe.wait_ge(k_lo_ready, 2)
            for t in range(KB0 // P):
                project_values(0, t, 0)
                project_values(0, t, 1)
            pe.wait_ge(q_landed, STACKED)
            score_pair(0, 0, 0)
            score_pair(0, 0, 2)

            period(0, 0)
            with pe.Fori(0, LOOP_PERIODS) as i:
                period(2 * i + 1, 1)
                period(2 * i + 2, 0)
            period(NB - 2, (NB - 2) % 2, with_wo=True)
            pe.wait_ge(wo_ready, 1)
            pe.wait_ge(k_lo_ready, G * NB)
            pe.wait_ge(v_ready, tiles_before(NB))
            turn_weight(wo_q, ("k", "v")).then_inc(quant_turned, 1)
            last_period((NB - 1) % 2)

            def stay_warm(n, b):
                for _ in range(n):
                    nc.tensor.matmul(bank[b][:, :], woT[:, 0, 0:P], woT[:, 0, :], start=True, stop=True)

            pe.wait_ge(folded, NB)
            for g in range(G):
                tr = nc.tensor.transpose(bank["t0"][:, g * P:(g + 1) * P], acc[:, g, :], ident[:, :])
            tr.then_inc(pe_done, 1)
            stay_warm(14, "v")
            pe.wait_ge(dve_done, 1)
            view = bank["t1"][:, :].bitcast(BF16)
            for c in range(CC):
                tr = nc.tensor.transpose(view[:, c * T:(c + 1) * T], o_q[:, c * P:(c + 1) * P], ident_bf[:, :])
            tr.then_inc(pe_done, 1)
            pe.wait_ge(dve_done, 2)
            for c in range(CC):
                mm = nc.tensor.matmul(bank["s0"][:, :], o_qT[:, c, :], woT[:, c, :], start=(c == 0), stop=(c == CC - 1))
            mm.then_inc(pe_done, 1)

            def turn_x(src, b):
                for c in range(CC):
                    tr = nc.tensor.transpose(bank[b][:, c * T:(c + 1) * T], src[:, c * P:(c + 1) * P], ident[:, :])
                tr.then_inc(pe_done, 1)

            stay_warm(16, "v")
            pe.wait_ge(dve_done, 3)
            turn_x(t1, "t0")
            pe.wait_ge(dve_done, 4)
            pe.wait_ge(gla_landed, 16 * 5)
            pe.wait_ge(tail_landed, 16 * 7)
            for c in range(CC):
                mm = nc.tensor.matmul(bank["s0"][0:16, 0:T], w_kg1[:, c, :], xT[:, c, :], start=(c == 0), stop=(c == CC - 1))
            mm.then_inc(pe_done, 1)

            def project_gla(w, b):
                for m in range(GKT):
                    for c in range(CC):
                        mm = nc.tensor.matmul(bank[b][:, m * T:(m + 1) * T], w[:, c, m * P:(m + 1) * P], xT[:, c, :],
                                              start=(c == 0), stop=(c == CC - 1))
                return mm

            project_gla(w_gq, "k")
            pe.wait_ge(act_done, 2)
            nc.tensor.matmul(bank["s1"][:, 0:C // 2], t2[0:16, 0:T], w_kg2[:, :], start=True, stop=True)\
              .then_inc(pe_done, 1)
            project_gla(w_gk, "v").then_inc(pe_done, 1)
            for c in range(CC):
                mm = nc.tensor.matmul(bank["o"][:, :], xT[:, c, :], w_gv[:, c, :], start=(c == 0), stop=(c == CC - 1))
            mm.then_inc(pe_done, 1)
            pe.wait_ge(dve_done, 5)
            for m in range(GKT):
                mm = nc.tensor.matmul(bank["t1"][:, m * T:(m + 1) * T], t0[:, m * P:(m + 1) * P], upper_sb[:, :],
                                      start=True, stop=True)
            mm.then_inc(pe_done, 1)

            def project_gate(chunks):
                for c in chunks:
                    mm = nc.tensor.matmul(bank["a"][:, :], xT[:, c, :], w_gg[:, c, :], start=(c == 0), stop=(c == CC - 1))
                return mm

            project_gate(range(2))
            pe.wait_ge(dve_done, 6)
            for h in range(GH):
                r = (h * GK) % P
                m = h * GK // P
                at = ["s0", "s1", "t0", "t1"][h % 4]
                mm = nc.tensor.matmul(bank[at][:, m * T:(m + 1) * T], t2[r:r + GK, C // 2 + m * T:C // 2 + (m + 1) * T],
                                      t2[r:r + GK, m * T:(m + 1) * T], start=True, stop=True)
            mm.then_inc(pe_done, 1)
            project_gate(range(2, CC)).then_inc(pe_done, 1)
            pe.wait_ge(pool_done, 1)
            pe.wait_ge(dve_done, 7)
            for h in range(GH):
                mm = nc.tensor.matmul(bank["k"][:, h * GV:(h + 1) * GV], at_sb[:, h, :], v_gla[:, h * GV:(h + 1) * GV],
                                      start=True, stop=True)
            mm.then_inc(pe_done, 1)
            stay_warm(18, "v")
            pe.wait_ge(dve_done, 8)
            turn_x(t0, "v")
            pe.wait_ge(dve_done, 9)
            for c in range(CC):
                mm = nc.tensor.matmul(bank["o"][:, :], xT[:, c, :], w_go[:, c, :], start=(c == 0), stop=(c == CC - 1))
            mm.then_inc(pe_done, 1)

            stay_warm(10, "v")
            pe.wait_ge(dve_done, 10)
            turn_x(t1, "t0")
            pe.wait_ge(dve_done, 11)
            for c in range(CC):
                mm = nc.tensor.matmul(bank["t1"][:, 0:E], xT[:, c, :], gate_sb[:, c, :], start=(c == 0), stop=(c == CC - 1))
            mm.then_inc(pe_done, 1)
            pe.wait_ge(dve_done, 12)

            def up(e):
                pe.wait_ge(up_lo_ready, e + 1)
                if e >= 2:
                    pe.wait_ge(act_ready, e - 1)
                hi = up_hi[e % 3][:, :, :].rearrange("p n (c i) -> p n c i", c=CC)
                lo = experts_lo[e % EXPERT_SLOTS][:, 0:2, :].rearrange("p n (c i) -> p n c i", c=CC)
                for c in range(CC):
                    for n, (a, b) in enumerate(((x_hiT, hi), (x_loT, hi), (x_hiT, lo))):
                        mm = nc.tensor.matmul(ps_s[e % 2][:, :], a[:, c, :], b[:, :, c, :],
                                              start=(c == 0 and n == 0), stop=(c == CC - 1 and n == 2))
                mm.then_inc(up_done, 1)

            def turn_act(e):
                pe.wait_ge(act_ready, e + 1)
                b = bank["k" if e % 2 == 0 else "v"]
                if e >= 2:
                    pe.wait_ge(act_kept, e - 1)
                for n in range(I // P):
                    tr = nc.tensor.transpose(b[:, n * T:(n + 1) * T], act_e[e % 2][:, n * P:(n + 1) * P], ident[:, :])
                tr.then_inc(act_turned, 1)

            def down(e):
                pe.wait_ge(act_kept, e + 1)
                pe.wait_ge(down_lo_ready, e + 1)
                hi = down_hi[e % 3][:, :].rearrange("p (c i) -> p c i", c=I // P)
                lo = experts_lo[e % EXPERT_SLOTS][:, 2, :].rearrange("p (c i) -> p c i", c=I // P)
                for c in range(I // P):
                    for n, (a, b) in enumerate(((act_hiT, hi), (act_loT, hi), (act_hiT, lo))):
                        mm = nc.tensor.matmul(bank["a"][:, :], a[e % 2][:, c, :], b[:, c, :],
                                              start=(e == 0 and c == 0 and n == 0),
                                              stop=(e == E - 1 and c == I // P - 1 and n == 2))
                mm.then_inc(down_done, 1)

            for e in range(E + 2):
                if e < E:
                    up(e)
                if 1 <= e <= E:
                    turn_act(e - 1)
                if e >= 2:
                    down(e - 2)

        @block.scalar
        def _(act):
            def split(s, half, slot, c):
                width = KB0 if isinstance(s, int) and s == 0 else KB
                nc.scalar.activation(c_hi[slot][:, c, 0:width], raw[slot][:, c, 0:width], ACT.Copy)\
                  .then_inc(ctx_hi_ready, 1)

            def keys_hi(s, g):
                width = KB0 if isinstance(s, int) and s == 0 else KB
                act.wait_ge(k_projected, G * s + g + 1)
                if g >= 2 or not (isinstance(s, int) and s == 0):
                    act.wait_ge(k_landed[(g - 2) % 4], STACKED * (s + 1) if g >= 2 else STACKED * s)
                nc.scalar.activation(k_hi[g % 2][:, 0:width], keys_bank(s, g), ACT.Identity,
                                     bias=bk_c[:, g:g + 1]).then_inc(k_hi_ready, 1)

            def exponentials(s, g, j, slot):
                width = KB0 if isinstance(s, int) and s == 0 else KB
                h = HG * g + j
                act.wait_ge(masked, H * s + h + 1)
                at = prob[:, h % SLOTS, 0:width]
                nc.scalar.activation(at, at, ACT.Exp, bias=neg_max[slot][:, h:h + 1], scale=-1.0,
                                     accum_out=row_sum[slot][:, h:h + 1]).then_inc(prob_ready, 1)

            def keep(s, g, t):
                n = tiles_before(s) * G + g * block_tiles(s) + t
                act.wait_ge(turned, n + 1)
                nc.scalar.activation(probT[:, t, :], ps_t[t % 2][:, :], ACT.Copy)\
                  .then_inc(kept_even if t % 2 == 0 else kept_odd, 1)

            def period(p, half, parity, project=True, split_next=True):
                nt = block_tiles(p)
                for q in range(G):
                    s, g = (p, q + 1) if q < 3 else (p + 1, 0)
                    slot = parity if q < 3 else (parity + 1) % 2
                    scores = q < 3 or project
                    if split_next:
                        if q == 1:
                            act.wait_ge(k_projected, G * (p + 1))
                            act.wait_ge(v_projected, tiles_before(p) + nt)
                            act.wait_ge(ctx_landed[parity], 16 * (half + 2))
                        for c in CHUNKS_IN[q]:
                            split(p + 2, None, parity, c)
                    if q == 3:
                        if not (isinstance(p, int) and p == 0):
                            act.wait_ge(folded, p)
                        act.wait_ge(drop_ready, (H // 2) * (p + 1))
                        nc.scalar.activation(rescale_w[:, :, :], drop[:, :].unsqueeze(2).to_broadcast([P, H, D]),
                                             ACT.Exp).then_inc(rescale_ready, 1)
                    if scores:
                        exponentials(s, g, 0, slot)
                        exponentials(s, g, 1, slot)
                    keep(p, q, 0)
                    if project:
                        keys_hi(p + 1, q)
                    if scores:
                        exponentials(s, g, 2, slot)
                        exponentials(s, g, 3, slot)
                    if nt > 2:
                        keep(p, q, 2)
                    if not project:
                        keep(p, q, 3)

            act.wait_ge(dve_chain, 3)
            nc.scalar.activation(col[:, 3:4], col[:, 2:3], ACT.Sqrt).then_inc(act_done, 1)
            act.wait_ge(ctx_landed[0], 16)
            for c in range(CC):
                split(0, 0, 0, c)
            act.wait_ge(wk_landed, 16)
            for c in range(CC):
                nc.scalar.activation(wk_hi[:, c, :], wk_nat[:, c, :], ACT.Copy).then_inc(w_hi_ready, 1)
            act.wait_ge(wv_landed, 16)
            for c in range(CC):
                nc.scalar.activation(wv_hi[:, c, :], wv_nat[:, c, :], ACT.Copy).then_inc(w_hi_ready, 1)
            act.wait_ge(bias_landed, 16 * 4)
            for g in range(3):
                keys_hi(0, g)
            act.wait_ge(ctx_landed[1], 16)
            for c in range(2):
                split(1, 0, 1, c)
            act.wait_ge(q_ready, 1)
            nc.scalar.activation(q_hi[:, :, :], q_sb[:, :, :], ACT.Copy).then_inc(q_hi_ready, 1)
            for c in range(2, CC):
                split(1, 0, 1, c)
            keys_hi(0, 3)
            for j in range(HG):
                exponentials(0, 0, j, 0)

            period(0, 0, 0)
            with act.Fori(0, LOOP_PERIODS) as i:
                period(2 * i + 1, i, 1)
                period(2 * i + 2, i + 1, 0)
            period(NB - 2, (NB - 2) // 2, (NB - 2) % 2, split_next=False)
            act.wait_ge(quant_turned, 3)
            nc.scalar.activation(woT[:, 2:4, :].rearrange("p c o -> p (c o)"), bank["v"][:, :].bitcast(BF16),
                                 ACT.Copy).then_inc(wo_kept, 1)
            period(NB - 1, (NB - 1) // 2, (NB - 1) % 2, project=False, split_next=False)

            def up_high(e):
                act.wait_ge(expert_landed[e % EXPERT_SLOTS], 48 * (e // EXPERT_SLOTS + 1))
                if e >= 3:
                    act.wait_ge(up_done, e - 2)
                nc.scalar.activation(up_hi[e % 3][:, :, :], experts_at[e % EXPERT_SLOTS][:, 0:2, :],
                                     ACT.Copy).then_inc(up_hi_ready, 1)

            def down_high(e):
                if e >= 3:
                    act.wait_ge(down_done, e - 2)
                nc.scalar.activation(down_hi[e % 3][:, :], experts_at[e % EXPERT_SLOTS][:, 2, :],
                                     ACT.Copy).then_inc(down_hi_ready, 1)

            act.wait_ge(var_ready, 1)
            nc.scalar.activation(col[:, 3:4], col[:, 2:3], ACT.Sqrt).then_inc(std_ready, 1)
            act.wait_ge(folded, NB)
            up_high(0)
            act.wait_ge(pe_done, 5)
            nc.scalar.activation(t2[0:16, 0:T], bank["s0"][0:16, 0:T], ACT.Copy).then_inc(act_done, 1)
            act.wait_ge(abs_ready, 1)
            nc.scalar.activation(t3[:, 0:C // 2], t3[:, 0:C // 2], ACT.Exp, scale=-1.0).then_inc(exp_neg, 1)
            act.wait_ge(exp_neg, 1)
            nc.scalar.activation(t3[:, 0:C // 2], t3[:, 0:C // 2], ACT.Ln, bias=one_c).then_inc(ln_ready, 1)
            act.wait_ge(pe_done, 9)
            nc.scalar.activation(t1[:, 0:C // 2], bank["t1"][:, 0:C // 2], ACT.Exp).then_inc(decay_ready, 1)
            nc.scalar.activation(t1[:, C // 2:C], bank["t1"][:, 0:C // 2], ACT.Exp, scale=-1.0).then_inc(decay_ready, 1)
            up_high(1)
            act.wait_ge(gate_ready, 1)
            nc.scalar.activation(t3[:, :], t3[:, :], ACT.Silu).then_inc(silu_ready, 1)
            act.wait_ge(var_ready, 2)
            nc.scalar.activation(small[:, 1, 0:GH], small[:, 0, 0:GH], ACT.Sqrt).then_inc(std_ready, 1)
            down_high(0)
            act.wait_ge(var_ready, 3)
            nc.scalar.activation(col[:, 3:4], col[:, 2:3], ACT.Sqrt).then_inc(std_ready, 1)
            act.wait_ge(dve_done, 11)
            nc.scalar.activation(x_hiT[:, :, :], xT[:, :, :], ACT.Copy)\
              .then_inc(x_hi_ready, 1)
            act.wait_ge(logit_ready, 1)
            nc.scalar.activation(small[:, 2, :], small[:, 0, :], ACT.Exp, bias=col[:, 10:11],
                                 accum_out=col[:, 11:12]).then_inc(route_ready, 1)
            for e in range(E + 1):
                if e + 2 < E:
                    up_high(e + 2)
                if e < E:
                    act.wait_ge(up_done, e + 1)
                    if e >= 2:
                        act.wait_ge(act_ready, e - 1)
                    nc.scalar.activation(silu_e[e % 2][:, :], ps_s[e % 2][:, 0:I], ACT.Silu).then_inc(silu_done, 1)
                if 1 <= e < E:
                    down_high(e)
                if e >= 1:
                    act.wait_ge(act_turned, e)
                    if e >= 3:
                        act.wait_ge(down_done, e - 2)
                    nc.scalar.activation(act_hiT[(e - 1) % 2][:, :, :].rearrange("p c t -> p (c t)"),
                                         bank["k" if e % 2 == 1 else "v"][:, 0:I], ACT.Copy).then_inc(act_hi_ready, 1)

        @block.gpsimd
        def _(pool):
            def split(s, slot, c):
                width = KB0 if isinstance(s, int) and s == 0 else KB
                pool.wait_ge(ctx_hi_ready, CC * s + c + 1)
                nc.gpsimd.tensor_tensor(c_lo[slot][:, c, 0:width], raw[slot][:, c, 0:width],
                                        c_hi[slot][:, c, 0:width].bitcast(F32), ALU.subtract)\
                  .then_inc(ctx_lo_ready, 1)

            def period(p, half, parity):
                for q in range(G):
                    for c in CHUNKS_IN[q]:
                        split(p + 2, parity, c)

            for c in range(CC):
                split(0, 0, c)
            for n, (hi, lo, src) in enumerate(((wk_hi, wk_lo, wk_nat), (wv_hi, wv_lo, wv_nat))):
                for c in range(CC):
                    pool.wait_ge(w_hi_ready, CC * n + c + 1)
                    nc.gpsimd.tensor_tensor(lo[:, c, :], src[:, c, :], hi[:, c, :].bitcast(F32),
                                            ALU.subtract).then_inc(w_lo_ready, 1)
            for c in range(CC):
                split(1, 1, c)
            period(0, 0, 0)
            with pool.Fori(0, LOOP_PERIODS) as i:
                period(2 * i + 1, i, 1)
                period(2 * i + 2, i + 1, 0)
            pool.wait_ge(scores_kept, 4)
            nc.gpsimd.affine_select(out=at_sb[:, :, :], in_=at_sb[:, :, :], compare_op=ALU.is_ge, fill=0.0,
                                    base=0, pattern=[[0, GH], [1, T]], channel_multiplier=-1).then_inc(pool_done, 1)
            for e in range(E):
                pool.wait_ge(down_hi_ready, e + 1)
                nc.gpsimd.tensor_tensor(experts_lo[e % EXPERT_SLOTS][:, 2, :], experts_at[e % EXPERT_SLOTS][:, 2, :],
                                        down_hi[e % 3][:, :].bitcast(F32), ALU.subtract)\
                  .then_inc(down_lo_ready, 1)

        @block.vector
        def _(dve):
            chained = [0]

            def link(ins):
                chained[0] += 1
                ins.then_inc(dve_chain, 1)
                dve.wait_ge(dve_chain, chained[0])

            def variance(src):
                link(nc.vector.bn_stats(stats[:, :], src))
                link(nc.vector.bn_aggr(col[:, 0:2], stats[:, :]))
                return nc.vector.tensor_scalar(col[:, 2:3], col[:, 1:2], EPS_LN, None, ALU.add)

            def normalise(dst, src):
                link(nc.vector.reciprocal(col[:, 4:5], col[:, 3:4]))
                return nc.vector.tensor_scalar(dst, src, col[:, 0:1], col[:, 4:5], ALU.subtract, ALU.mult)

            def scales(scale, inverse, src, n):
                link(nc.vector.tensor_reduce(scale, src, AX.X, ALU.max, apply_absolute_value=True))
                link(nc.vector.tensor_scalar(scale, scale, 1.0 / QMAX, EPS_Q, ALU.mult, ALU.max))
                link(nc.vector.reciprocal(inverse, scale))

            def rounded(dst, tmp):
                link(nc.vector.tensor_scalar(tmp, tmp, -ROUND, QMAX, ALU.add, ALU.min))
                return nc.vector.tensor_scalar(dst, tmp, -QMAX, None, ALU.max)

            def weight(scale, inverse, w_nat, w_rnd, w_q):
                scales(scale, inverse, w_nat[:, :, :], CC)
                for k in range(CC):
                    ins = nc.vector.tensor_scalar(w_rnd[:, k, :], w_nat[:, k, :], inverse[:, k:k + 1], ROUND,
                                                  ALU.mult, ALU.add)
                link(ins)
                nc.vector.memset(col[:, 9:10], 0.0).then_inc(wq_free, 1)
                return rounded(w_q, w_rnd[:, :, :])

            def keys_lo(s, g):
                width = KB0 if isinstance(s, int) and s == 0 else KB
                dve.wait_ge(k_hi_ready, G * s + g + 1)
                if g >= 2 or not (isinstance(s, int) and s == 0):
                    dve.wait_ge(k_landed[(g - 2) % 4], STACKED * (s + 1) if g >= 2 else STACKED * s)
                nc.vector.scalar_tensor_tensor(out=k_lo[g % 2][:, 0:width], in0=keys_bank(s, g),
                                               scalar=bk_c[:, g:g + 1], in1=k_hi[g % 2][:, 0:width].bitcast(F32),
                                               op0=ALU.add, op1=ALU.subtract).then_inc(k_lo_ready, 1)

            def values(s, t, slot):
                dve.wait_ge(v_projected, tiles_before(s) + t + 1)
                nc.vector.tensor_tensor(v_sb[slot][:, t, :], values_bank(s, t), bv_b[:, :], ALU.add)\
                  .then_inc(v_ready, 1)

            def mask_pair(s, g, j, slot, half):
                width = KB0 if isinstance(s, int) and s == 0 else KB
                n = H * s + HG * g + j
                if j == 0 and g == 0:
                    dve.wait_ge(mask_landed[slot], 16 * (half + 1))
                if j == 0 and not (isinstance(s, int) and s == 0 and g < 2):
                    dve.wait_ge(turned, turned_before(s, g))
                dve.wait_ge(scored, n + 2)
                if not (isinstance(n, int) and n == 0):
                    dve.wait_ge(masked, n)
                    if (g, j) == (0, 2) and not (isinstance(s, int) and s == 0):
                        dve.wait_ge(rescale_ready, s)
                    ph = (HG * g + j - 2) % H
                    now, old = (slot, 1 - slot) if (g, j) != (0, 0) else (1 - slot, slot)
                    nc.vector.tensor_tensor(drop[:, ph:ph + 2], neg_max[now][:, ph:ph + 2],
                                            neg_max[old][:, ph:ph + 2], ALU.subtract).then_inc(drop_ready, 1)
                for h in (HG * g + j, HG * g + j + 1):
                    nc.vector.tensor_tensor_reduce(out=prob[:, h % SLOTS, 0:width], in0=score_bank(s, h)[:, 0:width],
                                                   in1=mask_sb[slot][:, 0:width], scale=-1.0,
                                                   scalar=neg_max[1 - slot][:, h:h + 1], op0=ALU.add, op1=ALU.min,
                                                   accum_out=neg_max[slot][:, h:h + 1]).then_inc(masked, 1)

            def turned_before(s, g):
                if g >= 2:
                    return tiles_before(s) * G + (g - 1) * block_tiles(s)
                if isinstance(s, int) and s == 1:
                    return (G + g - 1) * (KB0 // P)
                return tiles_before(s) * G - (1 - g) * NT

            def keep(s, g, t):
                n = tiles_before(s) * G + g * block_tiles(s) + t
                dve.wait_ge(turned, n + 1)
                nc.vector.tensor_copy(probT[:, t, :], ps_t[1][:, :]).then_inc(kept_odd, 1)

            def fold(s, slot):
                dve.wait_ge(prob_ready, H * (s + 1))
                flat = acc[:, :, :].rearrange("p g t -> p (g t)")
                dve.wait_ge(rescale_turned, s + 1)
                nc.vector.tensor_tensor(l_sum[:, :], l_sum[:, :], rescale_w[:, :, 0], ALU.mult).then_inc(scaled, 1)
                nc.vector.tensor_tensor(flat, flat, bank["a"][:, :], ALU.mult).then_inc(scaled, 1)
                dve.wait_ge(scaled, 2 * s + 2)
                nc.vector.tensor_tensor(l_sum[:, :], l_sum[:, :], row_sum[slot][:, :], ALU.add)
                dve.wait_ge(group_applied, G * (s + 1))
                nc.vector.tensor_tensor(flat, flat, bank["o"][:, :], ALU.add).then_inc(folded, 1)

            def wo_step(q, part):
                scale, inverse = col[:, 12:16], col[:, 16:20]
                if (q, part) == (0, 1):
                    dve.wait_ge(wo_landed, 16)
                    nc.vector.tensor_reduce(scale[:, 0:2], wo_nat[:, 0:2, :], AX.X, ALU.max, apply_absolute_value=True)
                elif (q, part) == (1, 0):
                    link(nc.vector.tensor_reduce(scale[:, 2:4], wo_nat[:, 2:4, :], AX.X, ALU.max,
                                                 apply_absolute_value=True))
                    link(nc.vector.tensor_scalar(scale, scale, 1.0 / QMAX, EPS_Q, ALU.mult, ALU.max))
                    link(nc.vector.reciprocal(inverse, scale))
                elif (q, part) in ((1, 1), (2, 0)):
                    for k in (0, 1) if q == 1 else (2, 3):
                        ins = nc.vector.tensor_scalar(wo_rnd[:, k, :], wo_nat[:, k, :], inverse[:, k:k + 1], ROUND,
                                                      ALU.mult, ALU.add)
                    link(ins)
                elif (q, part) == (2, 1):
                    link(nc.vector.tensor_scalar(wo_rnd[:, :, :], wo_rnd[:, :, :], -ROUND, QMAX, ALU.add, ALU.min))
                    for k in range(CC):
                        ins = nc.vector.tensor_copy(wo_scale_w[:, k, :], scale[:, k:k + 1].to_broadcast([P, P]))
                    ins.then_inc(wo_scale_ready, 1)
                elif (q, part) == (3, 0):
                    nc.vector.tensor_scalar(wo_q, wo_rnd[:, :, :], -QMAX, None, ALU.max).then_inc(wo_ready, 1)
                    dve.wait_ge(wo_scale_turned, 1)
                    nc.vector.tensor_copy(wo_scale_b[:, :], bank["a"][:, :]).then_inc(wo_scale_kept, 1)

            def period(p, half, parity, project=True, with_wo=False):
                nt = block_tiles(p)
                for q in range(G):
                    s, g = (p, q + 1) if q < 3 else (p + 1, 0)
                    slot = parity if q < 3 else 1 - parity
                    mhalf = half if q < 3 else (half if parity == 0 else half + 1)
                    scores = q < 3 or project
                    if scores:
                        mask_pair(s, g, 0, slot, mhalf)
                    elif q == 3:
                        last_drop()
                    pair_first = not project and 0 < q < 3
                    if pair_first:
                        mask_pair(s, g, 2, slot, mhalf)
                    if q > 0 or not project:
                        keep(p, q, 1)
                    if q == 0 and not (isinstance(p, int) and p == 0):
                        fold(p - 1, 1 - parity)
                    if q == 0 and project:
                        keep(p, q, 1)
                    if scores and not pair_first:
                        mask_pair(s, g, 2, slot, mhalf)
                    if project:
                        keys_lo(p + 1, q)
                    if with_wo:
                        wo_step(q, 0)
                    if nt > 2 and project:
                        keep(p, q, 3)
                    if project:
                        values(p + 1, q, 1 - parity)
                    if with_wo:
                        wo_step(q, 1)

            def last_drop():
                s = NB - 1
                dve.wait_ge(masked, H * NB)
                nc.vector.tensor_tensor(drop[:, H - 2:H], neg_max[s % 2][:, H - 2:H], neg_max[1 - s % 2][:, H - 2:H],
                                        ALU.subtract).then_inc(drop_ready, 1)

            dve.wait_ge(x_landed, 16)
            link(variance(x_sb[:, :]))
            nc.vector.memset(neg_max[1][:, :], BIG).then_inc(init_ready, 1)
            nc.vector.memset(l_sum[:, :], 0.0).then_inc(init_ready, 1)
            nc.vector.memset(acc[:, :, :], 0.0).then_inc(init_ready, 1)
            dve.wait_ge(act_done, 1)
            link(normalise(x_norm[:, :], x_sb[:, :]))
            scales(col[:, 5:6], col[:, 6:7], x_norm[:, :], 1)
            link(nc.vector.tensor_scalar(x_norm[:, :], x_norm[:, :], col[:, 6:7], ROUND, ALU.mult, ALU.add))
            link(rounded(xq[:, :], x_norm[:, :]))
            dve.wait_ge(const_landed, 16)
            nc.vector.tensor_copy(x_scale_w[:, :], col[:, 5:6].to_broadcast([P, P])).then_inc(quant_ready, 1)
            nc.vector.tensor_copy(ident_bf[:, :], ident[:, :]).then_inc(ident_ready, 1)
            dve.wait_ge(wq_landed, 16)
            weight(col[:, 12:16], col[:, 16:20], wq_nat, wq_rnd, wq_q[:, :, :]).then_inc(quant_ready, 1)
            dve.wait_ge(bias_landed, 16 * 4)
            keys_lo(0, 0)
            dve.wait_ge(quant_turned, 1)
            nc.vector.tensor_copy(xqT[:, :, :].rearrange("p c t -> p (c t)"),
                                  bank["t0"][:, :].bitcast(BF16)[:, 0:C]).then_inc(turned_kept, 1)
            nc.vector.tensor_copy(x_scale_b, bank["t1"][:, 0:T])

            def keep_weight(dst, banks):
                nc.vector.tensor_copy(dst[:, 0:2, :].rearrange("p c o -> p (c o)"), bank[banks[0]][:, :].bitcast(BF16))
                return nc.vector.tensor_copy(dst[:, 2:4, :].rearrange("p c o -> p (c o)"),
                                             bank[banks[1]][:, :].bitcast(BF16))

            dve.wait_ge(quant_turned, 2)
            keep_weight(wqT, ("s0", "s1")).then_inc(turned_kept, 1)
            keys_lo(0, 1)
            dve.wait_ge(q_made, 1)
            for g in range(G):
                ins = nc.vector.scalar_tensor_tensor(out=q_sb[:, g, :], in0=bank["t0"][:, g * T:(g + 1) * T],
                                                     scalar=col[:, 12 + g:13 + g], in1=x_scale_b, op0=ALU.mult, op1=ALU.mult)
            link(ins)
            for g in range(G):
                ins = nc.vector.tensor_scalar(q_sb[:, g, :], q_sb[:, g, :], bq_c[:, g:g + 1], float(D) ** -0.5,
                                              ALU.add, ALU.mult)
            ins.then_inc(q_ready, 1)
            dve.wait_ge(q_hi_ready, 1)
            nc.vector.tensor_tensor(q_lo[:, :, :], q_sb[:, :, :], q_hi[:, :, :].bitcast(F32), ALU.subtract)\
              .then_inc(q_lo_ready, 1)
            keys_lo(0, 2)
            dve.wait_ge(w_lo_ready, 2 * CC)
            mask_pair(0, 0, 0, 0, 0)
            mask_pair(0, 0, 2, 0, 0)
            for t in range(KB0 // P):
                values(0, t, 0)
            keys_lo(0, 3)

            period(0, 0, 0)
            with dve.Fori(0, LOOP_PERIODS) as i:
                period(2 * i + 1, i, 1)
                period(2 * i + 2, i + 1, 0)
            period(NB - 2, (NB - 2) // 2, (NB - 2) % 2, with_wo=True)
            dve.wait_ge(quant_turned, 3)
            nc.vector.tensor_copy(woT[:, 0:2, :].rearrange("p c o -> p (c o)"), bank["k"][:, :].bitcast(BF16))\
              .then_inc(wo_kept, 1)
            period(NB - 1, (NB - 1) // 2, (NB - 1) % 2, project=False)
            nc.vector.tensor_tensor(x_sb[:, :], x_sb[:, :], bo_b[:, :], ALU.add)
            fold(NB - 1, (NB - 1) % 2)

            dve.wait_ge(folded, NB)
            link(nc.vector.reciprocal(col[:, 24:24 + H], l_sum[:, :]))
            dve.wait_ge(pe_done, 1)
            link(nc.vector.tensor_tensor(t0[:, :].rearrange("p (h d) -> p h d", h=H),
                                         bank["t0"][:, :].rearrange("p (h d) -> p h d", h=H),
                                         col[:, 24:24 + H].unsqueeze(2).to_broadcast([P, H, D]), ALU.mult))
            scales(col[:, 5:6], col[:, 6:7], t0[:, :], 1)
            link(nc.vector.tensor_scalar(t0[:, :], t0[:, :], col[:, 6:7], ROUND, ALU.mult, ALU.add))
            rounded(o_q[:, :], t0[:, :]).then_inc(dve_done, 1)
            dve.wait_ge(pe_done, 2)
            nc.vector.tensor_copy(o_qT[:, :, :].rearrange("p c t -> p (c t)"),
                                  bank["t1"][:, :].bitcast(BF16)[:, 0:C]).then_inc(dve_done, 1)
            dve.wait_ge(pe_done, 3)
            link(nc.vector.scalar_tensor_tensor(out=t0[:, :], in0=bank["s0"][:, :], scalar=col[:, 5:6],
                                                in1=wo_scale_b[:, :], op0=ALU.mult, op1=ALU.mult))
            link(nc.vector.tensor_tensor(x_sb[:, :], x_sb[:, :], t0[:, :], ALU.add))

            variance(x_sb[:, :]).then_inc(var_ready, 1)
            nc.vector.memset(one_c, 1.0)
            dve.wait_ge(std_ready, 1)
            normalise(t1[:, :], x_sb[:, :]).then_inc(dve_done, 1)
            dve.wait_ge(pe_done, 4)
            nc.vector.tensor_copy(xT[:, :, :].rearrange("p c t -> p (c t)"), bank["t0"][:, :]).then_inc(dve_done, 1)

            def up_low(e):
                dve.wait_ge(up_hi_ready, e + 1)
                nc.vector.tensor_tensor(experts_lo[e % EXPERT_SLOTS][:, 0:2, :], experts_at[e % EXPERT_SLOTS][:, 0:2, :],
                                        up_hi[e % 3][:, :, :].bitcast(F32), ALU.subtract)\
                  .then_inc(up_lo_ready, 1)

            up_low(0)
            dve.wait_ge(pe_done, 6)
            dve.wait_ge(tail_landed, 16 * 7)
            HC = C // 2
            link(nc.vector.tensor_tensor(t0[:, 0:HC], bank["s1"][:, 0:HC], bkg2_b[:, :], ALU.add))
            nc.vector.scalar_tensor_tensor(out=t3[:, 0:HC], in0=t0[:, 0:HC], scalar=-1.0, in1=t0[:, 0:HC],
                                           op0=ALU.mult, op1=ALU.max).then_inc(abs_ready, 1)
            dve.wait_ge(abs_ready, 1)
            link(nc.vector.tensor_scalar(t0[:, 0:HC], t0[:, 0:HC], 0.0, 1.0 / 16.0, ALU.min, ALU.mult))
            dve.wait_ge(ln_ready, 1)
            nc.vector.scalar_tensor_tensor(out=t0[:, 0:HC], in0=t3[:, 0:HC], scalar=-1.0 / 16.0, in1=t0[:, 0:HC],
                                           op0=ALU.mult, op1=ALU.add).then_inc(dve_done, 1)
            dve.wait_ge(decay_ready, 2)
            dve.wait_ge(pe_done, 7)
            nc.vector.tensor_tensor(t2[:, 0:HC], bank["k"][:, 0:HC], t1[:, 0:HC], ALU.mult)
            nc.vector.scalar_tensor_tensor(out=t2[:, HC:C], in0=bank["v"][:, 0:HC], scalar=float(GV) ** -0.5,
                                           in1=t1[:, HC:C], op0=ALU.mult, op1=ALU.mult).then_inc(dve_done, 1)
            heads = lambda t: t[:, :].rearrange("p (h d) -> p h d", h=GH)
            wide = lambda c: c.unsqueeze(2).to_broadcast([P, GH, GV])
            dve.wait_ge(pe_done, 8)
            link(nc.vector.tensor_reduce(small[:, 0, 0:GH], heads(bank["o"]), AX.X, ALU.add))
            link(nc.vector.tensor_scalar(small[:, 0, 0:GH], small[:, 0, 0:GH], 1.0 / GV, None, ALU.mult))
            nc.vector.tensor_tensor(heads(v_gla), heads(bank["o"]), wide(small[:, 0, 0:GH]), ALU.subtract)\
              .then_inc(dve_done, 1)
            dve.wait_ge(pe_done, 10)
            for r, at in enumerate(("s0", "s1", "t0", "t1")):
                dst = at_sb[:, :, :].rearrange("p (m r) t -> p m r t", r=4)[:, :, r, :]
                nc.vector.tensor_copy(dst, bank[at][:, 0:GKT * T].rearrange("p (m t) -> p m t", m=GKT))\
                  .then_inc(scores_kept, 1)
            dve.wait_ge(pe_done, 11)
            nc.vector.tensor_tensor(t3[:, :], bank["a"][:, :], bg_b[:, :], ALU.add).then_inc(gate_ready, 1)
            up_low(1)
            dve.wait_ge(pe_done, 12)
            link(nc.vector.tensor_copy(t0[:, :], bank["k"][:, :]))
            link(nc.vector.tensor_tensor(t1[:, :], t0[:, :], t0[:, :], ALU.mult))
            link(nc.vector.tensor_reduce(small[:, 0, 0:GH], heads(t1), AX.X, ALU.add))
            nc.vector.tensor_scalar(small[:, 0, 0:GH], small[:, 0, 0:GH], 1.0 / GV, EPS_LN, ALU.mult, ALU.add)\
              .then_inc(var_ready, 1)
            dve.wait_ge(silu_ready, 1)
            link(nc.vector.tensor_tensor(t0[:, :], t0[:, :], t3[:, :], ALU.mult))
            dve.wait_ge(std_ready, 2)
            link(nc.vector.reciprocal(small[:, 2, 0:GH], small[:, 1, 0:GH]))
            nc.vector.tensor_tensor(heads(t0), heads(t0), wide(small[:, 2, 0:GH]), ALU.mult).then_inc(dve_done, 1)
            dve.wait_ge(pe_done, 13)
            nc.vector.tensor_copy(xT[:, :, :].rearrange("p c t -> p (c t)"), bank["v"][:, :]).then_inc(dve_done, 1)
            dve.wait_ge(pe_done, 14)
            link(nc.vector.tensor_tensor(x_sb[:, :], x_sb[:, :], bank["o"][:, :], ALU.add))

            variance(x_sb[:, :]).then_inc(var_ready, 1)
            dve.wait_ge(std_ready, 3)
            normalise(t1[:, :], x_sb[:, :]).then_inc(dve_done, 1)
            dve.wait_ge(pe_done, 15)
            nc.vector.tensor_copy(xT[:, :, :].rearrange("p c t -> p (c t)"), bank["t0"][:, :]).then_inc(dve_done, 1)
            dve.wait_ge(x_hi_ready, 1)
            nc.vector.tensor_tensor(x_loT[:, :, :], xT[:, :, :], x_hiT[:, :, :].bitcast(F32), ALU.subtract)\
              .then_inc(dve_done, 1)
            dve.wait_ge(pe_done, 16)
            link(nc.vector.tensor_copy(small[:, 0, :], bank["t1"][:, 0:E]))
            nc.vector.tensor_reduce(col[:, 10:11], small[:, 0, :], AX.X, ALU.max, negate=True).then_inc(logit_ready, 1)
            dve.wait_ge(route_ready, 1)
            link(nc.vector.reciprocal(col[:, 12:13], col[:, 11:12]))
            link(nc.vector.tensor_scalar(small[:, 2, :], small[:, 2, :], col[:, 12:13], None, ALU.mult))
            link(nc.vector.max(small[:, 3, 0:8], small[:, 2, :]))
            link(nc.vector.max_index(top_ids[:, :], small[:, 3, 0:8], small[:, 2, :]))
            link(nc.vector.tensor_copy(small[:, 4, 0:8], top_ids[:, :]))
            link(nc.vector.tensor_tensor(col[:, 13:14], small[:, 3, 0:1], small[:, 3, 1:2], ALU.add))
            link(nc.vector.tensor_scalar(col[:, 13:14], col[:, 13:14], 1e-20, None, ALU.add))
            link(nc.vector.reciprocal(col[:, 14:15], col[:, 13:14]))
            link(nc.vector.tensor_scalar(small[:, 3, 0:2], small[:, 3, 0:2], col[:, 14:15], None, ALU.mult))
            for n in range(2):
                ins = nc.vector.tensor_scalar(small[:, 5 + n, :], ids_sb[:, :], small[:, 4, n:n + 1],
                                              small[:, 3, n:n + 1], ALU.is_equal, ALU.mult)
            link(ins)
            link(nc.vector.tensor_tensor(small[:, 7, :], small[:, 5, :], small[:, 6, :], ALU.add))

            def keep_act(e):
                dve.wait_ge(act_hi_ready, e + 1)
                if e >= 2:
                    dve.wait_ge(down_done, e - 1)
                nc.vector.tensor_tensor(act_loT[e % 2][:, :, :].rearrange("p c t -> p (c t)"),
                                        bank["k" if e % 2 == 0 else "v"][:, 0:I],
                                        act_hiT[e % 2][:, :, :].rearrange("p c t -> p (c t)").bitcast(F32),
                                        ALU.subtract).then_inc(act_kept, 1)

            for e in range(E + 1):
                if e + 2 < E:
                    up_low(e + 2)
                if e < E:
                    dve.wait_ge(silu_done, e + 1)
                    if e >= 2:
                        dve.wait_ge(act_turned, e - 1)
                    nc.vector.scalar_tensor_tensor(out=act_e[e % 2][:, :], in0=silu_e[e % 2][:, :],
                                                   scalar=small[:, 7, e:e + 1], in1=ps_s[e % 2][:, I:2 * I],
                                                   op0=ALU.mult, op1=ALU.mult).then_inc(act_ready, 1)
                if e >= 1:
                    keep_act(e - 1)
            dve.wait_ge(down_done, E)
            nc.vector.tensor_tensor(t0[:, :], bank["a"][:, :], x_sb[:, :], ALU.add).then_inc(out_ready, 1)


def kernel(**inputs):
    import numpy as np
    import concourse.bacc as bacc
    from concourse import mybir as _mybir
    from concourse.bass_utils import run_bass_kernel_spmd as run

    a = {k: np.asarray(v) for k, v in inputs.items()}
    ctx = a["ctx_2048"][0]
    by_d = lambda w: w.reshape(G, HG, D, -1).transpose(0, 2, 1, 3).reshape(C, -1)
    chunks = lambda w: w.reshape(CC, P, -1).transpose(1, 0, 2)
    arrays = {
        "x": a["x"][0],
        "ctx_first": chunks(ctx[:KB0].T),
        "ctx_rest": ctx[KB0:].reshape(NB - 1, KB, CC, P).transpose(0, 3, 2, 1),
        "mask": a["mask_BxSxS2_ff0"][0],
        "wq": chunks(by_d(a["L0_xattn_wq"])),
        "bq": by_d(a["L0_xattn_bq"]).reshape(G, P).T,
        "wkT": chunks(by_d(a["L0_xattn_wk"]).T),
        "bk": by_d(a["L0_xattn_bk"]).reshape(G, P).T,
        "wvT": chunks(a["L0_xattn_wv"].T),
        "bv": a["L0_xattn_bv"],
        "wo": chunks(a["L0_xattn_wo"]),
        "bo": a["L0_xattn_bo"],
        "g_wq": a["L0_attn_Wq"],
        "g_wk": a["L0_attn_Wk"],
        "g_wkg1": chunks(a["L0_attn_Wkg1"]),
        "g_wkg2": a["L0_attn_Wkg2"],
        "g_bkg2": a["L0_attn_bkg2"],
        "g_wv": a["L0_attn_Wv"],
        "g_wg": a["L0_attn_Wg"],
        "g_bg": a["L0_attn_bg"],
        "g_wo": a["L0_attn_Wo"],
        "gateT": chunks(a["L0_ffn_gate_w"].T),
        "wg": a["L0_ffn_wg"],
        "wu": a["L0_ffn_wu"],
        "wd": a["L0_ffn_wd"],
        "eye": np.eye(P, dtype=np.float32),
        "upper": np.triu(np.ones((P, P), np.float32)),
        "expert_ids": np.arange(E, dtype=np.float32),
    }
    arrays = {k: np.ascontiguousarray(v) for k, v in arrays.items()}
    nc = bacc.Bacc("TRN2", target_bir_lowering=False, num_devices=1)
    aps = {k: nc.dram_tensor(f"in_{k}", v.shape, _mybir.dt.from_np(v.dtype), kind="ExternalInput").ap()
           for k, v in arrays.items()}
    out = nc.dram_tensor("out_y", (T, C), _mybir.dt.float32, kind="ExternalOutput").ap()
    perceiver_kernel(nc, **aps, out=out)
    r = run(nc, [{f"in_{k}": v for k, v in arrays.items()}], core_ids=[0])
    return r.results[0]["out_y"].reshape(1, T, C)
```
